# Optimizing a Trainium2 kernel written in Bass

```python
import numpy as np
import jax
import jax.numpy as jnp

def _softmax(x, axis=-1):
    return jax.nn.softmax(x, axis=axis)

def _gelu(x):
    return jax.nn.gelu(x, approximate=True)

def _silu(x):
    return jax.nn.silu(x)

def _sigmoid(x):
    return jax.nn.sigmoid(x)

def _layernorm(x, axis=-1, eps=1e-05):
    m = jnp.mean(x, axis=axis, keepdims=True)
    v = jnp.var(x, axis=axis, keepdims=True)
    return (x - m) / jnp.sqrt(v + eps)

def _scatter_add(tgt, idx, src, axis=0):
    return tgt.at[idx].add(src)

def _segment_sum(src, seg, n):
    return jax.ops.segment_sum(src, seg, n)
kernel_name = 'mk_gnn_preln_d4_gnn_r8_fb2dea'

def setup_inputs(seed: int=0):
    np.random.seed(seed)
    _w = jnp.asarray

    def _rec_inputs():
        import jax
        import jax.numpy as jnp
        _gk = jax.random.key(seed)
        x = -0.000202 + 1 * jax.random.normal(jax.random.fold_in(_gk, 1), (12500, 128), jnp.float32)
        _s = jax.random.randint(jax.random.fold_in(_gk, 2), (100000,), 0, 12500, jnp.int32)
        _d = jax.random.randint(jax.random.fold_in(_gk, 3), (100000,), 0, 12500, jnp.int32)
        _loop = jnp.arange(12500, dtype=jnp.int32)
        src = jnp.concatenate([_s, _d, _loop])
        dst = jnp.concatenate([_d, _s, _loop])
        _o = jnp.argsort(dst, stable=True)
        src = src[_o]
        dst = dst[_o]
        edge_attr_20 = jax.random.uniform(jax.random.fold_in(_gk, 12), (212500, 20), jnp.float32, 0.0, 1)
        edge_attr_42 = 0.000171677 + 1.0001 * jax.random.normal(jax.random.fold_in(_gk, 13), (212500, 42), jnp.float32)
        edge_type_3 = jax.random.randint(jax.random.fold_in(_gk, 15), (212500,), 0, 3, jnp.int32)
        edge_weight = jax.random.uniform(jax.random.fold_in(_gk, 16), (212500,), jnp.float32, 0.0, 0.999998)
        node_vec = jax.random.uniform(jax.random.fold_in(_gk, 17), (12500,), jnp.float32, 0.0, 0.999994)
        return (x, src, dst, edge_attr_20, edge_attr_42, edge_type_3, edge_weight, node_vec)
    x, src, dst, edge_attr_20, edge_attr_42, edge_type_3, edge_weight, node_vec = _rec_inputs()

    def _L0_gnn_setup():
        import jax, jax.numpy as jnp
        import numpy as np
        NODE_EMB_DIM = 16
        NUM_REL = 10

        def _rgcn_layer(x, src, dst, edge_type, w_rel, root, bias):
            N = x.shape[0]
            seg = dst * NUM_REL + edge_type
            xs = x[src]
            sums = jax.ops.segment_sum(xs, seg, num_segments=N * NUM_REL)
            cnt = jax.ops.segment_sum(jnp.ones(seg.shape, x.dtype), seg, num_segments=N * NUM_REL)
            mean = (sums / jnp.maximum(cnt, 1.0)[:, None]).reshape(N, NUM_REL, -1)
            return jnp.einsum('nrd,rdo->no', mean, w_rel) + x @ root + bias
        key = jax.random.key(seed)
        ks = jax.random.split(key, 10)
        N, E, C = (6250, 100000, 128)
        s = 1.0 / np.sqrt(C).astype(np.float32)
        x = jax.random.normal(ks[0], (N, C), jnp.float32)
        last_update = jax.random.uniform(ks[1], (N,), jnp.float32)
        t = jax.random.uniform(ks[2], (E,), jnp.float32)
        msg = jax.random.normal(ks[3], (E, 2 * NODE_EMB_DIM + NUM_REL), jnp.float32)
        w_rel1 = jax.random.normal(ks[4], (NUM_REL, C, C), jnp.float32) * s
        root1 = jax.random.normal(ks[5], (C, C), jnp.float32) * s
        b1 = jnp.zeros((C,), jnp.float32)
        w_rel2 = jax.random.normal(ks[6], (NUM_REL, C, C), jnp.float32) * s
        root2 = jax.random.normal(ks[7], (C, C), jnp.float32) * s
        b2 = jnp.zeros((C,), jnp.float32)
        edge_index = jax.random.randint(ks[8], (2, E), 0, N, dtype=jnp.int32)
        return dict(x=x, last_update=last_update, t=t, msg=msg, w_rel1=w_rel1, root1=root1, b1=b1, w_rel2=w_rel2, root2=root2, b2=b2, edge_index=edge_index)
    _L0_gnn_all = _L0_gnn_setup()
    _L0_gnn_in = {k: v for k, v in _L0_gnn_all.items() if k in ('w_rel1', 'root1', 'b1', 'w_rel2', 'root2', 'b2')}
    del _L0_gnn_all

    def _L1_gnn_setup():
        import jax, jax.numpy as jnp
        import numpy as np
        N_NODES = 6250
        N_EDGES = 100000
        IN_FEATS = 128
        OUT_FEATS = 128
        N_REL = 3
        key = jax.random.key(seed)
        k1, k2, k3, k4, k5, k6 = jax.random.split(key, 6)
        feature = jax.random.normal(k1, (N_NODES, IN_FEATS), dtype=jnp.float32)
        bound = float(np.sqrt(6.0 / IN_FEATS))
        weight = jax.random.uniform(k2, (N_REL, IN_FEATS, OUT_FEATS), dtype=jnp.float32, minval=-bound, maxval=bound)
        norm = jax.random.uniform(k3, (N_EDGES,), dtype=jnp.float32)
        src = jax.random.randint(k4, (N_EDGES,), 0, N_NODES)
        dst = jax.random.randint(k5, (N_EDGES,), 0, N_NODES)
        rel_type = jax.random.randint(k6, (N_EDGES,), 0, N_REL)
        return {'feature': feature, 'weight': weight, 'norm': norm, 'src': src, 'dst': dst, 'rel_type': rel_type}
    _L1_gnn_all = _L1_gnn_setup()
    _L1_gnn_in = {k: v for k, v in _L1_gnn_all.items() if k in ('weight',)}
    del _L1_gnn_all

    def _L2_gnn_setup():
        import jax, jax.numpy as jnp
        import numpy as np
        N_NODES = 12500
        N_EDGES = 200000
        D_IN = 128
        HIDDEN = 128
        EPS = 1e-05

        def _sage_conv(h, src, dst, n, Wl, bl, Wr):
            msg_sum = jax.ops.segment_sum(h[src], dst, num_segments=n)
            deg = jax.ops.segment_sum(jnp.ones((src.shape[0],), h.dtype), dst, num_segments=n)
            agg = msg_sum / jnp.maximum(deg, 1.0)[:, None]
            return agg @ Wl.T + bl + h @ Wr.T
        key = jax.random.key(seed)
        ks = jax.random.split(key, 12)
        glorot = lambda k, o, i: jax.random.normal(k, (o, i), jnp.float32) * (2.0 / (o + i)) ** 0.5
        return {'x': jax.random.normal(ks[0], (N_NODES, D_IN), jnp.float32), 'edge_index': jax.random.randint(ks[1], (2, N_EDGES), 0, N_NODES, jnp.int64), 'Wl1': glorot(ks[2], HIDDEN, D_IN), 'bl1': jnp.zeros((HIDDEN,), jnp.float32), 'Wr1': glorot(ks[3], HIDDEN, D_IN), 'Wl2': glorot(ks[4], HIDDEN, HIDDEN), 'bl2': jnp.zeros((HIDDEN,), jnp.float32), 'Wr2': glorot(ks[5], HIDDEN, HIDDEN), 'gamma': jnp.ones((HIDDEN,), jnp.float32), 'beta': jnp.zeros((HIDDEN,), jnp.float32), 'fcW': jax.random.uniform(ks[6], (HIDDEN, HIDDEN), jnp.float32, -1.0, 1.0) * (6.0 / (2 * HIDDEN)) ** 0.5, 'fcb': jnp.zeros((HIDDEN,), jnp.float32)}
    _L2_gnn_all = _L2_gnn_setup()
    _L2_gnn_in = {k: v for k, v in _L2_gnn_all.items() if k in ('Wl1', 'bl1', 'Wr1', 'Wl2', 'bl2', 'Wr2', 'gamma', 'beta', 'fcW', 'fcb')}
    del _L2_gnn_all

    def _L3_gnn_setup():
        import jax, jax.numpy as jnp
        import numpy as np
        N_ATOMS = 2500
        N_EDGES = 80000
        N_BASIS = 128
        N_RBF = 20
        N_FILT = 128

        def ssp(v):
            return jax.nn.softplus(v) - jnp.log(2.0).astype(v.dtype)
        key = jax.random.key(seed)
        ks = jax.random.split(key, 16)
        s = lambda fan_in: 1.0 / np.sqrt(fan_in)
        return {'x': jax.random.normal(ks[0], (N_ATOMS, N_BASIS), dtype=jnp.float32), 'f_ij': jax.random.uniform(ks[1], (N_EDGES, N_RBF), dtype=jnp.float32), 'rcut_ij': jax.random.uniform(ks[2], (N_EDGES,), dtype=jnp.float32), 'idx_i': jax.random.randint(ks[3], (N_EDGES,), 0, N_ATOMS), 'idx_j': jax.random.randint(ks[4], (N_EDGES,), 0, N_ATOMS), 'W_in2f': jax.random.normal(ks[5], (N_BASIS, N_FILT), dtype=jnp.float32) * s(N_BASIS), 'W_filt1': jax.random.normal(ks[6], (N_RBF, N_FILT), dtype=jnp.float32) * s(N_RBF), 'b_filt1': jnp.zeros((N_FILT,), dtype=jnp.float32), 'W_filt2': jax.random.normal(ks[7], (N_FILT, N_FILT), dtype=jnp.float32) * s(N_FILT), 'b_filt2': jnp.zeros((N_FILT,), dtype=jnp.float32), 'W_out1': jax.random.normal(ks[8], (N_FILT, N_BASIS), dtype=jnp.float32) * s(N_FILT), 'b_out1': jnp.zeros((N_BASIS,), dtype=jnp.float32), 'W_out2': jax.random.normal(ks[9], (N_BASIS, N_BASIS), dtype=jnp.float32) * s(N_BASIS), 'b_out2': jnp.zeros((N_BASIS,), dtype=jnp.float32)}
    _L3_gnn_all = _L3_gnn_setup()
    _L3_gnn_in = {k: v for k, v in _L3_gnn_all.items() if k in ('W_in2f', 'W_filt1', 'b_filt1', 'W_filt2', 'b_filt2', 'W_out1', 'b_out1', 'W_out2', 'b_out2')}
    del _L3_gnn_all
    return {'x': x, 'src': src, 'dst': dst, 'edge_attr_20': edge_attr_20, 'edge_attr_42': edge_attr_42, 'edge_type_3': edge_type_3, 'edge_weight': edge_weight, 'node_vec': node_vec, 'L0_gnn_w_rel1': _L0_gnn_in['w_rel1'], 'L0_gnn_root1': _L0_gnn_in['root1'], 'L0_gnn_b1': _L0_gnn_in['b1'], 'L0_gnn_w_rel2': _L0_gnn_in['w_rel2'], 'L0_gnn_root2': _L0_gnn_in['root2'], 'L0_gnn_b2': _L0_gnn_in['b2'], 'L1_gnn_weight': _L1_gnn_in['weight'], 'L2_gnn_Wl1': _L2_gnn_in['Wl1'], 'L2_gnn_bl1': _L2_gnn_in['bl1'], 'L2_gnn_Wr1': _L2_gnn_in['Wr1'], 'L2_gnn_Wl2': _L2_gnn_in['Wl2'], 'L2_gnn_bl2': _L2_gnn_in['bl2'], 'L2_gnn_Wr2': _L2_gnn_in['Wr2'], 'L2_gnn_gamma': _L2_gnn_in['gamma'], 'L2_gnn_beta': _L2_gnn_in['beta'], 'L2_gnn_fcW': _L2_gnn_in['fcW'], 'L2_gnn_fcb': _L2_gnn_in['fcb'], 'L3_gnn_W_in2f': _L3_gnn_in['W_in2f'], 'L3_gnn_W_filt1': _L3_gnn_in['W_filt1'], 'L3_gnn_b_filt1': _L3_gnn_in['b_filt1'], 'L3_gnn_W_filt2': _L3_gnn_in['W_filt2'], 'L3_gnn_b_filt2': _L3_gnn_in['b_filt2'], 'L3_gnn_W_out1': _L3_gnn_in['W_out1'], 'L3_gnn_b_out1': _L3_gnn_in['b_out1'], 'L3_gnn_W_out2': _L3_gnn_in['W_out2'], 'L3_gnn_b_out2': _L3_gnn_in['b_out2']}

def reference(x, src, dst, edge_attr_20, edge_attr_42, edge_type_3, edge_weight, node_vec, L0_gnn_w_rel1, L0_gnn_root1, L0_gnn_b1, L0_gnn_w_rel2, L0_gnn_root2, L0_gnn_b2, L1_gnn_weight, L2_gnn_Wl1, L2_gnn_bl1, L2_gnn_Wr1, L2_gnn_Wl2, L2_gnn_bl2, L2_gnn_Wr2, L2_gnn_gamma, L2_gnn_beta, L2_gnn_fcW, L2_gnn_fcb, L3_gnn_W_in2f, L3_gnn_W_filt1, L3_gnn_b_filt1, L3_gnn_W_filt2, L3_gnn_b_filt2, L3_gnn_W_out1, L3_gnn_b_out1, L3_gnn_W_out2, L3_gnn_b_out2):
    import jax
    import jax.numpy as jnp

    def _L0_gnn_ref(x, last_update, t, msg, w_rel1, root1, b1, w_rel2, root2, b2, edge_index):
        import jax, jax.numpy as jnp
        import numpy as np
        NODE_EMB_DIM = 16
        NUM_REL = 10

        def _rgcn_layer(x, src, dst, edge_type, w_rel, root, bias):
            N = x.shape[0]
            seg = dst * NUM_REL + edge_type
            xs = x[src]
            sums = jax.ops.segment_sum(xs, seg, num_segments=N * NUM_REL)
            cnt = jax.ops.segment_sum(jnp.ones(seg.shape, x.dtype), seg, num_segments=N * NUM_REL)
            mean = (sums / jnp.maximum(cnt, 1.0)[:, None]).reshape(N, NUM_REL, -1)
            return jnp.einsum('nrd,rdo->no', mean, w_rel) + x @ root + bias
        src, dst = (edge_index[0], edge_index[1])
        edge_type = jnp.argmax(msg[:, NODE_EMB_DIM:-NODE_EMB_DIM], axis=1).astype(jnp.int32)
        h = jax.nn.relu(_rgcn_layer(x, src, dst, edge_type, w_rel1, root1, b1))
        return _rgcn_layer(h, src, dst, edge_type, w_rel2, root2, b2)

    def _L1_gnn_ref(feature, weight, norm, src, dst, rel_type):
        import jax, jax.numpy as jnp
        import numpy as np
        N_NODES = 6250
        N_EDGES = 100000
        IN_FEATS = 128
        OUT_FEATS = 128
        N_REL = 3
        hr = jnp.einsum('ni,rio->rno', feature, weight)
        msg = hr[rel_type, src] * norm[:, None]
        h = jax.ops.segment_sum(msg, dst, num_segments=feature.shape[0])
        return jax.nn.relu(h)

    def _L2_gnn_ref(x, edge_index, Wl1, bl1, Wr1, Wl2, bl2, Wr2, gamma, beta, fcW, fcb):
        import jax, jax.numpy as jnp
        import numpy as np
        N_NODES = 12500
        N_EDGES = 200000
        D_IN = 128
        HIDDEN = 128
        EPS = 1e-05

        def _sage_conv(h, src, dst, n, Wl, bl, Wr):
            msg_sum = jax.ops.segment_sum(h[src], dst, num_segments=n)
            deg = jax.ops.segment_sum(jnp.ones((src.shape[0],), h.dtype), dst, num_segments=n)
            agg = msg_sum / jnp.maximum(deg, 1.0)[:, None]
            return agg @ Wl.T + bl + h @ Wr.T
        src, dst = (edge_index[0], edge_index[1])
        n = x.shape[0]
        h = jax.nn.relu(_sage_conv(x, src, dst, n, Wl1, bl1, Wr1))
        h = _sage_conv(h, src, dst, n, Wl2, bl2, Wr2)
        h = jax.nn.relu(h)
        mu = h.mean(axis=0)
        var = ((h - mu) ** 2).mean(axis=0)
        h = (h - mu) * jax.lax.rsqrt(var + EPS) * gamma + beta
        return h @ fcW.T + fcb

    def _L3_gnn_ref(x, f_ij, rcut_ij, idx_i, idx_j, W_in2f, W_filt1, b_filt1, W_filt2, b_filt2, W_out1, b_out1, W_out2, b_out2):
        import jax, jax.numpy as jnp
        import numpy as np
        N_ATOMS = 2500
        N_EDGES = 80000
        N_BASIS = 128
        N_RBF = 20
        N_FILT = 128

        def ssp(v):
            return jax.nn.softplus(v) - jnp.log(2.0).astype(v.dtype)
        n_atoms = x.shape[0]
        h = x @ W_in2f
        Wij = ssp(f_ij @ W_filt1 + b_filt1) @ W_filt2 + b_filt2
        Wij = Wij * rcut_ij[:, None]
        x_ij = h[idx_j] * Wij
        agg = jax.ops.segment_sum(x_ij, idx_i, num_segments=n_atoms)
        out = ssp(agg @ W_out1 + b_out1) @ W_out2 + b_out2
        return out
    edge_index = jnp.stack([src, dst])
    h = jnp.maximum(_layernorm(x, axis=-1), 0.0)
    x = x + _L0_gnn_ref(h, node_vec, edge_weight, edge_attr_42, L0_gnn_w_rel1, L0_gnn_root1, L0_gnn_b1, L0_gnn_w_rel2, L0_gnn_root2, L0_gnn_b2, edge_index)
    h = jnp.maximum(_layernorm(x, axis=-1), 0.0)
    x = x + _L1_gnn_ref(h, L1_gnn_weight, edge_weight, src, dst, edge_type_3)
    h = jnp.maximum(_layernorm(x, axis=-1), 0.0)
    x = x + _L2_gnn_ref(h, edge_index, L2_gnn_Wl1, L2_gnn_bl1, L2_gnn_Wr1, L2_gnn_Wl2, L2_gnn_bl2, L2_gnn_Wr2, L2_gnn_gamma, L2_gnn_beta, L2_gnn_fcW, L2_gnn_fcb)
    h = jnp.maximum(_layernorm(x, axis=-1), 0.0)
    x = x + _L3_gnn_ref(h, edge_attr_20, edge_weight, src, dst, L3_gnn_W_in2f, L3_gnn_W_filt1, L3_gnn_b_filt1, L3_gnn_W_filt2, L3_gnn_b_filt2, L3_gnn_W_out1, L3_gnn_b_out1, L3_gnn_W_out2, L3_gnn_b_out2)
    return x

_drawn_inputs = setup_inputs


def setup_inputs(seed=0):
    import zlib

    import numpy as np

    out = dict(_drawn_inputs(seed))
    spreads = {'L0_gnn_b1': (0.0, 0.1),
     'L0_gnn_b2': (0.0, 0.303),
     'L2_gnn_bl1': (0.0, 0.1),
     'L2_gnn_bl2': (0.0, 0.1),
     'L2_gnn_gamma': (1.0, 0.2),
     'L2_gnn_beta': (0.0, 0.411),
     'L2_gnn_fcb': (0.0, 0.444),
     'L3_gnn_b_filt1': (0.0, 0.1),
     'L3_gnn_b_filt2': (0.0, 0.1),
     'L3_gnn_b_out1': (0.0, 0.8),
     'L3_gnn_b_out2': (0.0, 0.462)}
    factors = {}
    for name, (base, spread) in spreads.items():
        noise = np.random.default_rng([zlib.crc32(name.encode()), seed]).standard_normal(out[name].shape)
        drawn = base * np.exp(spread * noise) if base else spread * noise
        out[name] = jnp.asarray(drawn.astype(out[name].dtype))
    for name, factor in factors.items():
        out[name] = (out[name] * factor).astype(out[name].dtype)
    return out
```

```python
from contextlib import ExitStack

import numpy as np
import concourse.bass as bass
from concourse import mybir

F32 = mybir.dt.float32
I32 = mybir.dt.int32
ALU = mybir.AluOpType
ACT = mybir.ActivationFunctionType
AX = mybir.AxisListType
ENG = mybir.EngineType

P = 128
GROUP = 16
QUAD = 4
SB = 4 * P
EPS = 1e-5
BANK = 512
LANES = 2
COPIES = QUAD

DENSE = [
    dict(src="", upd="", ln=True, table="wrel", rels=10, root="root1", bias="b1_0", xin=0, xout=None),
    dict(src="relu", upd="", ln=False, table="wrel", rels=10, root="root2", bias="b1_1", xin=None, xout=None),
    dict(src="copy", upd="ident", ln=True, table="w1", rels=3, root="", xin=0, xout=1),
    dict(src="relu", upd="ident", ln=True, table="wl1", rels=1, root="wr1", bias="bl1", xin=1, xout=2),
    dict(src="relu", upd="", ln=False, table="wl2", rels=1, root="wr2", bias="bl2", xin=None, xout=None),
    dict(src="bn", upd="fcw", row="fcb", ln=True, table="win", rels=1, root="", xin=2, xout=3),
    dict(src="sum", upd="wout2", row="bout2", ln=False, table="", rels=0, root="", xin=3, xout=4),
]
NREL = 10
NCNT = NREL + 1
COUNT, LOOKUP, PLAIN, FILTER = range(4)
PASSES = [COUNT, LOOKUP, PLAIN, PLAIN, PLAIN, PLAIN, FILTER]
COLS = ["b1_0", "b1_1", "bl1", "bl2", "gamma", "beta", "bfilt1", "bout1"]
WEIGHTS = [("wrel", NREL * P), ("root1", P), ("root2", P), ("w1", 3 * P), ("wl1", P), ("wr1", P), ("wl2", P),
           ("wr2", P), ("fcw", P), ("win", P), ("wout1", P), ("wout2", P), ("wfilt2", P)]
ROWS = ["fcb", "bout2", "bfilt2"]


def build(nc, d, out, n_nodes, n_edges):
    nsb = -(-(n_nodes + P) // SB)
    nacc = nsb * SB
    ngroups = -(-n_edges // (GROUP * P))
    ntiles = ngroups * GROUP
    nwin = -(-n_nodes // P)
    bn_chunk = max(c for c in range(1, BANK + 1) if n_nodes % c == 0)
    n_feat = 20

    def turns(k, flag):
        return nsb * sum(bool(flag(p)) for p in DENSE[:k])

    def has_src(p): return p["src"] != ""
    def has_x(p): return p["xin"] is not None
    def has_xout(p): return p["xout"] is not None
    def has_upd(p): return p["upd"] != ""
    def has_ln(p): return p["ln"]
    def has_root(p): return p["root"] != ""
    def has_table(p): return p["rels"] > 0

    def cuts(p):
        return [(a, min(a + BANK, p["rels"] * P)) for a in range(0, p["rels"] * P, BANK)]

    def n_chunks(p):
        return 4 * len(cuts(p))

    def chunks(k):
        return nsb * sum(n_chunks(p) for p in DENSE[:k])

    with ExitStack() as ctx:
        def sb(name, shape, dt=F32):
            return ctx.enter_context(nc.sbuf_tensor(name, shape, dt))

        def sem(name):
            return ctx.enter_context(nc.semaphore(name))

        x_dram = [d["x"]] + [nc.dram_tensor(f"x{k}_dram", (nacc, P), F32).ap() for k in (1, 2, 3)] + [out]
        x_dram = [x.rearrange("(s j p) c -> p s j c", j=4, p=P) for x in x_dram]
        table_dram = {r: nc.dram_tensor(f"table{r}_dram", (nacc * r, P), F32).ap() for r in (NREL, 3, 1)}

        agg_dram = [nc.dram_tensor(f"agg{c}_dram", (nacc + P, P), F32).ap() for c in range(COPIES)]

        acc = sb("acc", [P, max(nacc, 2 * P * NREL)])
        scratch = sb("scratch", [P, max(nacc, 3 * GROUP * P + 6 * BANK)])
        src_i = sb("src_i", [P, ntiles], I32)
        row_i = sb("row_i", [P, ntiles + GROUP], I32)
        dst_i = sb("dst_i", [P, ntiles], I32)
        first_i = sb("first_i", [P, ntiles], I32)
        rel_dst = sb("rel_dst", [P, ntiles])
        win_i = sb("win_i", [1, ntiles], I32)
        etype = sb("etype", [P, ntiles])
        wt_a = sb("wt_a", [P, ntiles])
        wt_deg = sb("wt_deg", [P, ntiles])
        ident = sb("ident", [P, P])
        iota_i = sb("iota_i", [P, P], I32)
        iota = sb("iota", [P, P])
        ones = sb("ones", [P, P])
        sel_deg = sb("sel_deg", [NCNT, P])
        W = {n: sb(n, [P, w]) for n, w in WEIGHTS}
        W["ident"] = ident
        wfilt1 = sb("wfilt1", [n_feat, P])
        bias_row = {n: sb(n, [1, P]) for n in ROWS}
        cols = sb("cols", [P, len(COLS)])
        col = {n: cols[:, i:i + 1] for i, n in enumerate(COLS)}
        half = sb("half", [P, 1])
        zeros = sb("zeros", [P, P])
        lower = sb("lower", [P, P])
        dump = sb("dump", [P, 1])
        dump_i = sb("dump_i", [P, 1], I32)
        dup = sb("dup", [P, 3, GROUP])
        sum_row = sb("sum_row", [P, GROUP], I32)
        reps_f = sb("reps_f", [P, 6])
        reps_i = sb("reps_i", [P, 1], I32)
        general, fast = reps_f[:, 4:5], reps_f[:, 5:6]
        win0 = sb("win0", [P, 2])
        bn = sb("bn", [P, 8])
        bn_st = sb("bn_st", [P, n_nodes // bn_chunk, 6])

        xs = sb("xs", [P, 4, P])
        yT = sb("yT", [P, SB])
        xn = sb("xn", [P, 4, P])
        h = sb("h", [P, 4, P])
        hT_s = sb("hT_s", [P, SB])
        tab_s = sb("tab_s", [P, LANES, NREL * P])
        st = sb("st", [P, 4, 6])
        mv = sb("mv", [P, 4, 2])
        nrm = sb("nrm", [P, 4, 4])
        flat = lambda t: t[:, :, :].rearrange("p j c -> p (j c)")

        rows = sb("rows", [P, GROUP, P])
        hot = flat(tab_s)[:, 0:GROUP * P].rearrange("p (u n) -> p u n", u=GROUP)
        row_st = sb("row_st", [P, GROUP], I32)
        rw_st = sb("rw_st", [P, 2, GROUP])
        wout_st = sb("wout_st", [P, 2, GROUP])
        rel_hot = sb("rel_hot", [P, GROUP, NCNT])
        rev = sb("rev", [P, NREL])
        junk = xs
        rel_hotT = yT[0:NCNT, :]
        counts = scratch[0:NCNT, 0:nacc]
        msg = scratch[:, 0:GROUP * P].rearrange("p (u c) -> p u c", u=GROUP)
        same = hot
        src_row = scratch[:, 2 * GROUP * P + 6 * BANK:3 * GROUP * P + 6 * BANK].bitcast(I32).rearrange(
            "p (q e) -> p q e", q=4)
        sums = acc[:, 0:GROUP * P].rearrange("p (q b) -> p q b", q=4)
        agg_in = scratch[:, 0:COPIES * SB].rearrange("p (k j c) -> p k j c", k=COPIES, j=4)
        feat = scratch[0:n_feat, GROUP * P:2 * GROUP * P].rearrange("p (q e) -> p q e", q=4)
        f_buf = scratch[:, 2 * GROUP * P:2 * GROUP * P + 6 * BANK].rearrange("p (k b e) -> p k b e", k=3, b=2)
        attr = acc[:, 0:2 * P * NREL].rearrange("p (b t r) -> p b t r", b=2, r=NREL)

        ps = [ctx.enter_context(nc.psum_tensor(f"ps{k}", [P, BANK], F32)) for k in range(8)]

        loaded = sem("loaded")
        attr_in = [sem("attr_in0"), sem("attr_in1")]
        attr_used = sem("attr_used")
        made = sem("made")
        prep = sem("prep")
        bad_ready = sem("bad_ready")
        bad_sum = sem("bad_sum")
        reps_ready = sem("reps_ready")
        late_in = sem("late_in")
        wrel2_in = sem("wrel2_in")
        rows_ready = sem("rows_ready")
        win_ready = sem("win_ready")
        win_step = sem("win_step")
        row_staged = sem("row_staged")
        row_in = [sem(f"row_in{q}") for q in range(4)]
        rw_staged = sem("rw_staged")
        hot_made = sem("hot_made")
        deg_done = sem("deg_done")
        hot_ready = sem("hot_ready")
        mm_done = sem("mm_done")
        add_done = sem("add_done")
        rel_ready = sem("rel_ready")
        relT_mm = sem("relT_mm")
        relT_ready = sem("relT_ready")
        look_mm = sem("look_mm")
        inv_ready = sem("inv_ready")
        feat_in = [sem(f"feat_in{q}") for q in range(4)]
        f1_mm = sem("f1_mm")
        ssp_step = sem("ssp_step")
        ssp_parts = sem("ssp_parts")
        ssp_sum = sem("ssp_sum")
        filt_mm = sem("filt_mm")
        msg_ready = sem("msg_ready")
        src_in = [sem(f"src_in{q}") for q in range(4)]
        same_ready = sem("same_ready")
        dup_step = sem("dup_step")
        dest_ready = sem("dest_ready")
        scattered = [sem(f"scattered{j}") for j in range(COPIES)]
        sums_free = sem("sums_free")
        zeroed = sem("zeroed")
        agg_read = sem("agg_read")
        agg_step = sem("agg_step")
        aggT_mm = sem("aggT_mm")
        x_in = sem("x_in")
        y_copy = sem("y_copy")
        out_mm = sem("out_mm")
        out_parts = sem("out_parts")
        y_sum = sem("y_sum")
        y_ready = sem("y_ready")
        upd_mm = sem("upd_mm")
        x_new = sem("x_new")
        x_out = sem("x_out")
        st_ready = sem("st_ready")
        mv_ready = sem("mv_ready")
        rstd_ready = sem("rstd_ready")
        var_ready = sem("var_ready")
        sd_ready = sem("sd_ready")
        nrm_ready = sem("nrm_ready")
        h_ready = sem("h_ready")
        hT_mm = sem("hT_mm")
        hT_ready = sem("hT_ready")
        root_mm = sem("root_mm")
        acc_init = sem("acc_init")
        acc_zero = sem("acc_zero")
        tab_mm = sem("tab_mm")
        evac_a = sem("evac_a")
        evac_v = sem("evac_v")
        tab_out = [sem(f"tab_out{j}") for j in range(LANES)]
        bn_var = sem("bn_var")
        bn_sd = sem("bn_sd")
        bn_ready = sem("bn_ready")

        settled = sem("settled")

        n_loads = 3 + len(WEIGHTS) + 2 + len(ROWS)
        n_attr = -(-ntiles // P)

        def reps_of(e):
            e.wait_ge(reps_ready, 1)
            return e.value_load(reps_i[0:1, 0:1], min_val=1, max_val=nwin)

        def settle(e):
            e.sem_inc(settled, 1)

        def tiles_before(reps, pn):
            last = len(PASSES) - 1
            return reps * (min(pn, last) * ntiles) + (ntiles if pn > last else 0)

        def windows(e, g, q):
            return nc.values_load_multi_w_load_instructions(
                win_i[0:1, bass.ds(g * GROUP + QUAD * q, QUAD)], engines=[e.engine],
                min_val=0, max_val=n_nodes)[1]

        def lane_uses(k):
            return turns(k, has_table) * (4 // LANES)

        block = ctx.enter_context(nc.Block())

        @block.sync
        def _(sp):
            for dst, name in ([(src_i, "src"), (dst_i, "dst"), (first_i, "first")] + [(W[n], n) for n, _ in WEIGHTS]
                              + [(wfilt1, "wfilt1"), (cols, "cols")] + [(bias_row[n], n) for n in ROWS]):
                sp.dma_start(dst[:], d[name]).then_inc(loaded, 16)
            for c in range(n_attr):
                n = min(P, ntiles - c * P)
                if c >= 2:
                    sp.wait_ge(attr_used, c - 1)
                sp.dma_start(attr[:, c % 2, 0:n, :], d["attr"][:, c * P:c * P + n, :]).then_inc(attr_in[c % 2], 16)
            sp.wait_ge(made, 8)
            for agg in agg_dram:
                sp.dma_start(agg.rearrange("(r p) c -> p r c", p=P),
                             zeros[:, :].unsqueeze(1).broadcast_to([P, nsb * 4 + 1, P])).then_inc(zeroed, 16)
            reps = reps_of(sp)

            for k, p in enumerate(DENSE):
                if has_x(p):
                    sp.wait_ge(x_out, 16 * turns(k, has_xout))
                    with sp.Fori(0, nsb) as i:
                        if p["src"] == "sum":
                            sp.wait_ge(aggT_mm, i)
                            settle(sp)
                            for c in range(COPIES):
                                sp.dma_start(agg_in[:, c, :, :], agg_dram[c][0:nacc, :].rearrange(
                                    "(s j p) c -> p s j c", j=4, p=P)[:, bass.ds(i, 1)].rearrange("p s j c -> p (s j) c")
                                ).then_inc(agg_read, 16)
                        sp.wait_ge(x_new, i + turns(k, has_x))
                        sp.dma_start(xs[:], x_dram[p["xin"]][:, bass.ds(i, 1)].rearrange("p s j c -> p (s j) c")
                                     ).then_inc(x_in, 16)
                        if has_xout(p):
                            sp.wait_ge(x_new, i + (turns(k, has_x) + 1))
                            sp.dma_start(x_dram[p["xout"]][:, bass.ds(i, 1)].rearrange("p s j c -> p (s j) c"), xn[:]
                                         ).then_inc(x_out, 16)
                if k == 0:
                    sp.wait_ge(tab_mm, chunks(1))
                    sp.dma_start(W["wrel"][:], d["wrel2"]).then_inc(wrel2_in, 16)
                if k == 1:
                    sp.wait_ge(add_done, reps * (3 * ntiles) + GROUP)
                    sp.dma_start(etype[:, :].bitcast(I32), d["type"]).then_inc(late_in, 16)
                    sp.dma_start(wt_a[:], d["weight"]).then_inc(late_in, 16)
                if k == 5:
                    sp.wait_ge(add_done, tiles_before(reps, 6) + GROUP)
                    settle(sp)
                    with sp.Fori(0, ngroups) as g:
                        for q in range(4):
                            edges = bass.ds(g * (GROUP * P) + q * BANK, BANK)
                            sp.wait_ge(f1_mm, g * 4 + (q + 1))
                            sp.dma_start(feat[:, q, :], d["feat"][:, edges]).then_inc(feat_in[q], 16)
                            sp.wait_ge(same_ready, g * 4 + (q + 1))
                            sp.dma_start(src_row[:, q, :], d["src_row"][0:1, edges].broadcast_to([P, BANK])
                                         ).then_inc(src_in[q], 16)
                    for s in scattered:
                        sp.wait_ge(s, 16 * 4 * ngroups)
            sp.wait_ge(x_out, 16 * turns(len(DENSE), has_xout))

        @block.gpsimd
        def _(pool):
            pool.memset(ident[:], 0.0).then_inc(made, 1)
            pool.memset(sel_deg[:], 0.0).then_inc(made, 1)
            pool.memset(ones[:], 1.0).then_inc(made, 1)
            pool.memset(half[:], 0.5).then_inc(made, 1)
            pool.iota(iota_i[:], pattern=[[1, P]], base=0, channel_multiplier=0).then_inc(made, 1)
            pool.memset(zeros[:], 0.0).then_inc(made, 1)
            pool.memset(lower[:], 0.0).then_inc(made, 1)
            pool.iota(dump_i[:], pattern=[[0, 1]], base=nacc, channel_multiplier=1).then_inc(made, 1)
            pool.wait_ge(made, 8)
            pool.affine_select(out=ident[:], in_=ident[:], compare_op=ALU.not_equal, fill=1.0, base=0,
                               pattern=[[-1, P]], channel_multiplier=1).then_inc(made, 1)
            pool.affine_select(out=sel_deg[:], in_=sel_deg[:], compare_op=ALU.not_equal, fill=1.0, base=-NREL,
                               pattern=[[0, P]], channel_multiplier=1).then_inc(made, 1)
            pool.affine_select(out=lower[:], in_=lower[:], compare_op=ALU.is_ge, fill=1.0, base=0,
                               pattern=[[1, P]], channel_multiplier=-1).then_inc(made, 1)
            pool.memset(row_i[:, ntiles:ntiles + GROUP], 0).then_inc(made, 1)
            pool.sem_inc(sums_free, 2 * QUAD)
            reps = reps_of(pool)

            for k, p in enumerate(DENSE):
                if not has_table(p):
                    continue
                width = p["rels"] * P
                table = table_dram[p["rels"]].rearrange("(s j p r) c -> p s j (r c)", j=4, p=P, r=p["rels"])
                with pool.Fori(0, nsb) as i:
                    for j in range(4):
                        done = (j + 1) * len(cuts(p))
                        pool.wait_ge(evac_a, i * (n_chunks(p) // 2) + (2 + chunks(k) // 2 + (done + 1) // 2))
                        pool.wait_ge(evac_v, i * (n_chunks(p) // 2) + (2 + chunks(k) // 2 + done // 2))
                        pool.dma_start(table[:, bass.ds(i, 1), j, :].rearrange("p s w -> p (s w)"),
                                       tab_s[:, j % LANES, 0:width]).then_inc(tab_out[j % LANES], 16)
                for j in range(LANES):
                    pool.wait_ge(tab_out[j], 16 * lane_uses(k + 1))
                pool.wait_ge(rows_ready, sum(q in (0, 2, 3, 5) for q in range(k + 1)))
                if PASSES[k + 1] == FILTER:
                    pool.wait_ge(zeroed, 16 * COPIES)

                    def gather_quad(before, u0, column):
                        pool.wait_ge(msg_ready, before + 1)
                        pool.tensor_copy(row_st[:, u0:u0 + QUAD], row_i[:, column]).then_inc(row_staged, 1)
                        pool.wait_ge(row_staged, reps * (5 * 2 * ngroups) + before + 1)
                        settle(pool)
                        for u in range(u0, u0 + QUAD):
                            pool.indirect_dma_start(
                                rows[:, u, :], None, table_dram[p["rels"]],
                                bass.IndirectOffsetOnAxis(ap=row_st[:, u:u + 1], axis=0)).then_inc(row_in[u // QUAD], 16)

                    gather_quad(0, 0, slice(0, QUAD))
                    gather_quad(1, QUAD, slice(QUAD, 2 * QUAD))
                    with pool.Fori(0, ngroups) as g:
                        base = pool.snap(tiles_before(reps, 6) + g * GROUP)
                        for q in range(4):
                            gather_quad(g * 4 + (q + 2), (q + 2) % 4 * QUAD, bass.ds(g * GROUP + QUAD * (q + 2), QUAD))
                            pool.wait_ge(dest_ready, g * 4 + (q + 1))
                            pool.wait_ge(add_done, base + (GROUP + QUAD * (q + 1)))
                            for j in range(QUAD):
                                pool.wait_ge(scattered[j], g * 64 + 16 * q)
                                pool.sem_inc(sums_free, 1)
                                pool.indirect_dma_start(
                                    agg_dram[j], bass.IndirectOffsetOnAxis(ap=sum_row[:, QUAD * q + j:QUAD * q + j + 1], axis=0),
                                    sums[:, q, j * P:(j + 1) * P], None, compute_op=ALU.add).then_inc(scattered[j], 16)
                    for q in range(2):
                        pool.wait_ge(row_in[q], ((reps * 5) * ngroups + (ngroups + 1)) * 64)
                    continue
                with pool.Fori(0, reps) as r:
                    with pool.Fori(0, ngroups) as g:
                        turn = pool.snap(reps * (k * ngroups) + r * ngroups + g)
                        used = pool.snap(reps * ntiles + turn * GROUP)
                        for part in range(2):
                            pool.wait_ge(mm_done, used + (part + 1) * (GROUP // 2))
                            us = range(part * (GROUP // 2), (part + 1) * (GROUP // 2))
                            pool.tensor_copy(row_st[:, us[0]:us[-1] + 1],
                                             row_i[:, bass.ds(g * GROUP + us[0], GROUP // 2)]).then_inc(row_staged, 1)
                            pool.wait_ge(row_staged, turn * 2 + (part + 1))
                            settle(pool)
                            for u in us:
                                pool.indirect_dma_start(
                                    rows[:, u, :], None, table_dram[p["rels"]],
                                    bass.IndirectOffsetOnAxis(ap=row_st[:, u:u + 1], axis=0)
                                ).then_inc(row_in[u // QUAD], 16)

        @block.scalar
        def _(act):
            act.sem_inc(evac_a, 2)
            reps = reps_of(act)

            def softplus_terms(src, bias, a, b, sig, before):
                act.activation(a, src, ACT.Abs, bias=bias).then_inc(ssp_step, 1)
                act.activation(b, src, ACT.Relu, bias=bias)
                act.wait_ge(ssp_step, before + 1)
                act.activation(a, a, ACT.Exp, scale=-1.0).then_inc(ssp_step, 1)
                act.wait_ge(ssp_step, before + 2)
                act.activation(a, a, ACT.Ln, bias=half[:], scale=0.5).then_inc(sig, 1)

            for k, p in enumerate(DENSE):
                nck = n_chunks(p)
                hT = hT_s if has_ln(p) else yT
                act.wait_ge(add_done, tiles_before(reps, k + 1) + GROUP)
                if p["src"] == "bn":
                    act.wait_ge(bn_var, 1)
                    act.activation(bn[:, 3:4], bn[:, 2:3], ACT.Sqrt).then_inc(bn_sd, 1)
                    act.wait_ge(bn_ready, 1)
                with act.Fori(0, nsb) as i:
                    acc_i = acc[:, bass.ds(i * SB, SB)]
                    if has_upd(p) and p["src"] != "sum":
                        act.wait_ge(upd_mm, i + turns(k, has_upd))
                    elif has_src(p) and p["src"] != "sum":
                        act.wait_ge(tab_mm, i * nck + chunks(k))
                    settle(act)
                    if p["src"] == "copy":
                        act.activation(yT[:], acc_i, ACT.Copy).then_inc(y_ready, 1)
                    elif p["src"] == "relu":
                        act.activation(yT[:], acc_i, ACT.Relu).then_inc(y_ready, 1)
                    elif p["src"] == "bn":
                        act.activation(yT[:], acc_i, ACT.Identity, bias=bn[:, 6:7], scale=bn[:, 5:6]).then_inc(y_ready, 1)
                    elif p["src"] == "sum":
                        act.wait_ge(aggT_mm, i + 1)
                        act.wait_ge(out_mm, i)
                        act.activation(flat(h), ps[1][:], ACT.Copy).then_inc(y_copy, 1)
                        act.wait_ge(out_mm, i + 1)
                        act.wait_ge(y_sum, i)
                        softplus_terms(ps[7][:], col["bout1"], hT_s[:], tab_s[:, 0, 0:SB], out_parts,
                                       i * 2 + ngroups * 8)
                    if has_ln(p):
                        n = turns(k, has_ln)
                        act.wait_ge(var_ready, i + (n + 1))
                        act.activation(nrm[:, :, 1], nrm[:, :, 0], ACT.Sqrt).then_inc(sd_ready, 1)
                        act.wait_ge(nrm_ready, i + (n + 1))
                        for j in range(4):
                            a = act.activation(h[:, j, :], xn[:, j, :], ACT.Relu, bias=nrm[:, j, 3:4], scale=nrm[:, j, 2:3])
                        a.then_inc(h_ready, 1)
                        act.wait_ge(hT_mm, i + (n + 1))
                        act.wait_ge(tab_mm, i * nck + chunks(k))
                        act.activation(hT_s[:], ps[1][:], ACT.Copy).then_inc(hT_ready, 1)
                    if has_root(p):
                        act.wait_ge(root_mm, i + (turns(k, has_root) + 1))
                        settle(act)
                        act.activation(acc_i, ps[2][:], ACT.Identity, bias=col[p["bias"]]).then_inc(acc_init, 1)
                    if has_table(p):
                        for c in range(0, nck, 2):
                            j, cut = c // len(cuts(p)), cuts(p)[c % len(cuts(p))]
                            act.wait_ge(tab_mm, i * nck + (chunks(k) + c + 1))
                            act.wait_ge(tab_out[j % LANES], i * (16 * 4 // LANES) + 16 * (lane_uses(k) + j // LANES))
                            act.activation(tab_s[:, j % LANES, cut[0]:cut[1]], ps[3 + c % 4][:, 0:cut[1] - cut[0]],
                                           ACT.Copy).then_inc(evac_a, 1)
                if k + 1 < len(PASSES) and PASSES[k + 1] == LOOKUP:
                    with act.Fori(0, reps) as r:
                        with act.Fori(0, ngroups) as g:
                            for q in range(4):
                                n = (r * ngroups + g) * 4 + q
                                act.wait_ge(look_mm, n)
                                act.wait_ge(relT_mm, n + 1)
                                act.activation(rel_hotT, ps[4 + q % 2][0:NCNT, :], ACT.Copy).then_inc(relT_ready, 1)
                if k == 5:
                    with act.Fori(0, ngroups) as g:
                        base = act.snap(tiles_before(reps, 6) + g * GROUP)

                        def filter_terms(q):
                            n = act.snap(g * 4 + q)
                            act.wait_ge(ssp_sum, n + 1)
                            act.wait_ge(f1_mm, n + 5)
                            softplus_terms(ps[4 + q % 2][:], col["bfilt1"], f_buf[:, 0, q % 2, :],
                                           f_buf[:, 1, q % 2, :], ssp_parts, n * 2)

                        filter_terms(0)
                        filter_terms(1)
                        for q in range(4):
                            act.wait_ge(sums_free, g * 16 + 4 * q)
                            act.wait_ge(mm_done, base + (GROUP + QUAD * (q + 1)))
                            act.activation(sums[:, q, :], ps[q][:], ACT.Copy).then_inc(add_done, QUAD)
                            if q + 2 < 4:
                                filter_terms(q + 2)

        @block.tensor
        def _(pe):
            pe.wait_ge(made, 12)
            pe.wait_ge(loaded, 16 * n_loads)
            pe.wait_ge(bad_ready, 1)
            pe.matmul(ps[7][:, 0:1], ones[:], reps_f[:, 3:4], start=True, stop=True).then_inc(bad_sum, 1)
            pe.sem_inc(mm_done, GROUP)
            pe.sem_inc(f1_mm, 4)
            reps = reps_of(pe)

            def tile_products(base, q, lhs, m, rhs=hot):
                pe.wait_ge(add_done, base + QUAD * (q + 1))
                pe.wait_ge(hot_ready, base + QUAD * (q + 1))
                for u in range(QUAD * q, QUAD * (q + 1)):
                    j = u % QUAD
                    pe.matmul(ps[q][0:m, j * P:(j + 1) * P], lhs[:, u, :], rhs[:, u, :], start=True, stop=True
                              ).then_inc(mm_done, 1)

            def gathered(base, q):
                pe.wait_ge(row_in[q], base + 64)

            def run_pass(pn):
                kind = PASSES[pn]
                if kind == LOOKUP:
                    pe.wait_ge(inv_ready, 1)
                with pe.Fori(0, reps if kind != FILTER else 1) as r:
                    if kind == LOOKUP:
                        pe.wait_ge(win_ready, reps * pn + r + 1)
                        settle(pe)
                    with pe.Fori(0, ngroups) as g:
                        base = pe.snap(reps * (pn * ntiles) + r * ntiles + g * GROUP)
                        quads = pe.snap((r * ngroups + g) * 4)
                        if kind != COUNT:
                            landed = pe.snap(((reps * (pn - 1) + r) * ngroups + g) * 64)
                        if kind == COUNT:
                            pe.wait_ge(rel_ready, r * ngroups + g + 1)
                            for q in range(4):
                                tile_products(base, q, rel_hot, NCNT)
                        if kind == PLAIN:
                            for q in range(4):
                                gathered(landed, q)
                                tile_products(base, q, rows, P)
                        if kind == LOOKUP:
                            pe.wait_ge(rel_ready, (reps + r) * ngroups + g + 1)
                            for q in range(4):
                                for j in range(QUAD):
                                    mm = pe.matmul(ps[4 + q % 2][0:NCNT, j * P:(j + 1) * P], rel_hot[:, QUAD * q + j, :],
                                                   ident[:], start=True, stop=True)
                                mm.then_inc(relT_mm, 1)
                                win = windows(pe, g, q)
                                pe.wait_ge(hot_ready, base + QUAD * q)
                                pe.wait_ge(relT_ready, quads + (q + 1))
                                for j in range(QUAD):
                                    window = counts[:, bass.ds(win[j], P)]
                                    pe.matmul(ps[6][:, j * P:(j + 1) * P], rel_hotT[:, j * P:(j + 1) * P], window,
                                              start=True, stop=True)
                                    mm = pe.matmul(ps[7][:, j * P:(j + 1) * P], sel_deg[:], window, start=True, stop=True)
                                mm.then_inc(look_mm, 1)
                                gathered(landed, q)
                                tile_products(base, q, rows, P)
                        if kind == FILTER:
                            def first_product(q):
                                pe.wait_ge(feat_in[q], g * 16 + 16)
                                pe.matmul(ps[4 + q % 2][:], wfilt1[:], feat[:, q, :], start=True, stop=True).then_inc(f1_mm, 1)

                            first_product(0)
                            first_product(1)
                            for q in range(4):
                                pe.wait_ge(ssp_sum, quads + (q + 3))
                                for j in range(QUAD):
                                    o = ps[6 + q % 2][:, j * P:(j + 1) * P]
                                    pe.matmul(o, ones[0:1, :], bias_row["bfilt2"][:], start=True, stop=False)
                                    mm = pe.matmul(o, f_buf[:, 2, q % 2, j * P:(j + 1) * P], W["wfilt2"][:],
                                                   start=False, stop=True)
                                mm.then_inc(filt_mm, 1)
                                if q + 2 < 4:
                                    first_product(q + 2)
                                pe.wait_ge(msg_ready, quads + (q + 5))
                                tile_products(base, q, same, P, msg)

            run_pass(0)
            for k, p in enumerate(DENSE):
                nck = n_chunks(p)
                hT = hT_s if has_ln(p) else yT
                pe.wait_ge(add_done, tiles_before(reps, k + 1) + GROUP)
                settle(pe)
                if k == 1:
                    pe.wait_ge(wrel2_in, 16)
                with pe.Fori(0, nsb) as i:
                    if has_upd(p):
                        if p["src"] == "sum":
                            pe.wait_ge(agg_step, i * 3 + 3)
                            pe.wait_ge(y_copy, i)
                            for j in range(4):
                                mm = pe.matmul(ps[1][:, j * P:(j + 1) * P], agg_in[:, 0, j, :], ident[:], start=True, stop=True)
                            mm.then_inc(aggT_mm, 1)
                            pe.wait_ge(y_copy, i + 1)
                            pe.wait_ge(out_parts, i)
                            pe.matmul(ps[7][:], W["wout1"][:], flat(h), start=True, stop=True).then_inc(out_mm, 1)
                            pe.wait_ge(y_sum, i + 1)
                        else:
                            pe.wait_ge(y_ready, i + (turns(k, has_src) + 1))
                        pe.wait_ge(x_new, i + turns(k, has_x))
                        for j in range(4):
                            o = ps[0][:, j * P:(j + 1) * P]
                            if "row" in p:
                                pe.matmul(o, ones[0:1, :], bias_row[p["row"]][:], start=True, stop=False)
                            mm = pe.matmul(o, yT[:, j * P:(j + 1) * P], W[p["upd"]][:], start="row" not in p, stop=True)
                        mm.then_inc(upd_mm, 1)
                    if has_ln(p):
                        n = turns(k, has_ln)
                        pe.wait_ge(h_ready, i + (n + 1))
                        pe.wait_ge(hT_ready, i + n)
                        for j in range(4):
                            mm = pe.matmul(ps[1][:, j * P:(j + 1) * P], h[:, j, :], ident[:], start=True, stop=True)
                        mm.then_inc(hT_mm, 1)
                        pe.wait_ge(hT_ready, i + (n + 1))
                    elif has_table(p):
                        pe.wait_ge(y_ready, i + (turns(k, has_src) + 1))
                    if has_root(p):
                        pe.wait_ge(acc_init, i + turns(k, has_root))
                        pe.matmul(ps[2][:], W[p["root"]][:], hT[:], start=True, stop=True).then_inc(root_mm, 1)
                    for c in range(nck):
                        j, cut = c // len(cuts(p)), cuts(p)[c % len(cuts(p))]
                        pe.wait_ge((evac_a, evac_v)[c % 2], i * (nck // 2) + (chunks(k) // 2 + c // 2 + 1))
                        pe.matmul(ps[3 + c % 4][:, 0:cut[1] - cut[0]], hT[:, j * P:(j + 1) * P],
                                  W[p["table"]][:, cut[0]:cut[1]], start=True, stop=True).then_inc(tab_mm, 1)
                if has_table(p):
                    pe.wait_ge(evac_a, 2 + chunks(k + 1) // 2)
                    pe.wait_ge(evac_v, 2 + chunks(k + 1) // 2)
                    pe.wait_ge(acc_init, turns(k + 1, has_root))
                    pe.wait_ge(x_new, turns(k + 1, has_x))
                    run_pass(k + 1)

        @block.vector
        def _(dve):
            dve.sem_inc(evac_v, 2)
            steps = [0]

            def step(ins):
                steps[0] += 1
                ins.then_inc(prep, 1)
                dve.wait_ge(prep, steps[0])

            step(dve.memset(counts, 0.0))
            step(dve.memset(rel_hot[:], 1.0))
            step(dve.memset(wt_a[:], 0.0))
            step(dve.memset(wt_deg[:], 0.0))
            dve.wait_ge(made, 12)
            step(dve.tensor_copy(iota[:], iota_i[:]))
            step(dve.tensor_copy(dump[:], dump_i[:]))
            step(dve.tensor_scalar(rev[:], iota[:, 0:NREL], -1.0, float(NREL), ALU.mult, ALU.add))
            for c in range(n_attr):
                n = min(P, ntiles - c * P)
                a, best = attr[:, c % 2, 0:n, :], etype[:, c * P:c * P + n]
                dve.wait_ge(attr_in[c % 2], 16 * (c // 2 + 1))
                step(dve.tensor_reduce(best, a, AX.X, ALU.max))
                step(dve.tensor_tensor(a, a, best.unsqueeze(2).broadcast_to([P, n, NREL]), ALU.is_equal))
                step(dve.tensor_tensor(a, a, rev[:].unsqueeze(1).broadcast_to([P, n, NREL]), ALU.mult))
                dve.tensor_reduce(best, a, AX.X, ALU.max).then_inc(attr_used, 1)
            dve.wait_ge(attr_used, n_attr)
            step(dve.tensor_scalar(etype[:], etype[:], -1.0, float(NREL), ALU.mult, ALU.add))

            dve.wait_ge(loaded, 16 * n_loads)
            step(dve.tensor_tensor(rel_dst[:], dst_i[:], first_i[:], ALU.subtract))
            step(dve.tensor_reduce(reps_f[:, 0:1], rel_dst[:], AX.X, ALU.max))
            step(dve.tensor_reduce(reps_f[:, 1:2], rel_dst[:], AX.X, ALU.min))
            step(dve.tensor_scalar(reps_f[:, 0:1], reps_f[:, 0:1], P - 0.5, None, ALU.is_gt))
            step(dve.tensor_scalar(reps_f[:, 1:2], reps_f[:, 1:2], -0.5, None, ALU.is_lt))
            dve.tensor_tensor(reps_f[:, 3:4], reps_f[:, 0:1], reps_f[:, 1:2], ALU.add).then_inc(bad_ready, 1)
            dve.wait_ge(bad_sum, 1)
            step(dve.tensor_scalar(general, ps[7][:, 0:1], 1.0, None, ALU.min))
            step(dve.tensor_scalar(fast, general, -1.0, 1.0, ALU.mult, ALU.add))
            dve.tensor_scalar(reps_i[:], general, float(nwin - 1), 1.0, ALU.mult, ALU.add).then_inc(reps_ready, 1)
            dve.scalar_tensor_tensor(out=row_i[:, 0:ntiles], in0=src_i[:], scalar=float(NREL), in1=etype[:],
                                     op0=ALU.mult, op1=ALU.add).then_inc(rows_ready, 1)
            reps = reps_of(dve)
            dve.sem_inc(add_done, GROUP)
            dve.sem_inc(ssp_sum, 2)
            dve.sem_inc(msg_ready, 4)
            dve.sem_inc(same_ready, 4)

            def set_windows(pn, r):
                n = dve.snap((reps * pn + r) * 3)
                dve.tensor_tensor(win0[:, 1:2], win0[:, 0:1], general, ALU.mult).then_inc(win_step, 1)
                dve.wait_ge(win_step, n + 1)
                dve.tensor_scalar(rel_dst[:], first_i[:], fast, win0[:, 1:2], ALU.mult, ALU.add).then_inc(win_step, 1)
                dve.wait_ge(win_step, n + 2)
                dve.tensor_copy(win_i[:], rel_dst[0:1, :]).then_inc(win_ready, 1)
                dve.wait_ge(win_ready, reps * pn + r + 1)
                dve.tensor_tensor(rel_dst[:], dst_i[:], rel_dst[:], ALU.subtract)
                dve.tensor_scalar(win0[:, 0:1], win0[:, 0:1], float(P), None, ALU.add).then_inc(win_step, 1)
                dve.wait_ge(win_step, n + 3)
                settle(dve)

            def add_quad(base, g, q, target, m):
                win = windows(dve, g, q)
                dve.wait_ge(mm_done, base + (GROUP + QUAD * (q + 1)))
                for j in range(QUAD):
                    dve.wait_ge(add_done, base + (GROUP + QUAD * q + j))
                    window = target[:, bass.ds(win[j], P)]
                    dve.tensor_tensor(window, ps[q][0:m, j * P:(j + 1) * P], window, ALU.add).then_inc(add_done, 1)

            def run_pass(pn):
                kind = PASSES[pn]
                weights = {2: wt_a, 3: wt_a, 4: wt_deg, 5: wt_deg}.get(pn)
                step(dve.memset(win0[:, 0:1], 0.0))
                with dve.Fori(0, reps) as r:
                    set_windows(pn, r)
                    with dve.Fori(0, ngroups) as g:
                        turn = dve.snap((reps * pn + r) * ngroups + g)
                        base = dve.snap(turn * GROUP)
                        quads = dve.snap((r * ngroups + g) * 4)
                        dve.wait_ge(mm_done, base + GROUP)
                        dve.tensor_copy(rw_st[:, 0, :], rel_dst[:, bass.ds(g * GROUP, GROUP)]).then_inc(rw_staged, 1)
                        if kind in (COUNT, LOOKUP):
                            rel = etype[:, bass.ds(g * GROUP, GROUP)]
                            dve.tensor_copy(rw_st[:, 1, :], rel).then_inc(rw_staged, 1)
                            dve.wait_ge(rw_staged, turn * 2 + 2)
                            dve.tensor_tensor(rel_hot[:, :, 0:NREL], rw_st[:, 1, :].unsqueeze(2).broadcast_to([P, GROUP, NREL]),
                                              iota[:, 0:NREL].unsqueeze(1).broadcast_to([P, GROUP, NREL]), ALU.is_equal
                                              ).then_inc(rel_ready, 1)
                        else:
                            dve.tensor_copy(rw_st[:, 1, :], weights[:, bass.ds(g * GROUP, GROUP)]).then_inc(rw_staged, 1)
                            dve.wait_ge(rw_staged, turn * 2 + 2)

                        for u in range(GROUP):
                            if kind == PLAIN:
                                dve.tensor_scalar(hot[:, u, :], iota[:], rw_st[:, 0, u:u + 1], rw_st[:, 1, u:u + 1],
                                                  ALU.is_equal, ALU.mult).then_inc(hot_ready, 1)
                            else:
                                i = dve.tensor_scalar(hot[:, u, :], iota[:], rw_st[:, 0, u:u + 1], None, ALU.is_equal)
                                if kind == COUNT:
                                    i.then_inc(hot_ready, 1)
                                elif u == GROUP - 1:
                                    i.then_inc(hot_made, 1)
                        for q in range(4):
                            us = range(QUAD * q, QUAD * (q + 1))
                            if kind == LOOKUP:
                                dve.wait_ge(hot_made, r * ngroups + g + 1)
                                dve.wait_ge(look_mm, quads + (q + 1))
                                for w, bank in ((1, ps[7]), (0, ps[6])):
                                    for u in us:
                                        j = u % QUAD
                                        i = dve.tensor_tensor_reduce(
                                            out=(hot[:, u, :], junk[:, j, :])[w], in0=bank[:, j * P:(j + 1) * P],
                                            in1=hot[:, u, :], scale=1.0, scalar=0.0, op0=ALU.mult, op1=ALU.add,
                                            accum_out=wout_st[:, w, u:u + 1])
                                        if w == 0:
                                            i.then_inc(hot_ready, 1)
                                    if w == 1:
                                        i.then_inc(deg_done, 1)
                                        dve.wait_ge(deg_done, quads + (q + 1))
                            if kind == COUNT:
                                add_quad(base, g, q, counts, NCNT)
                            else:
                                add_quad(base, g, q, acc, P)
                        if kind == LOOKUP:
                            dve.wait_ge(hot_ready, base + GROUP)
                            for full, w in ((wt_a, 0), (wt_deg, 1)):
                                part = full[:, bass.ds(g * GROUP, GROUP)]
                                dve.tensor_tensor(part, wout_st[:, w, :], part, ALU.add)

            def filter_pass():
                turns_before = reps * (6 * ngroups)
                with dve.Fori(0, ngroups) as g:
                    base = dve.snap(tiles_before(reps, 6) + g * GROUP)
                    dve.wait_ge(dest_ready, g * 4)
                    dve.wait_ge(msg_ready, g * 4 + 4)
                    settle(dve)
                    dve.tensor_copy(rw_st[:, 0, :], src_i[:, bass.ds(g * GROUP, GROUP)]).then_inc(rw_staged, 1)
                    dve.tensor_copy(rw_st[:, 1, :], wt_a[:, bass.ds(g * GROUP, GROUP)]).then_inc(rw_staged, 1)
                    dve.wait_ge(rw_staged, (turns_before + g) * 2 + 2)

                    def terms_sum(q):
                        dve.wait_ge(ssp_parts, g * 4 + (q + 1))
                        dve.tensor_tensor(f_buf[:, 2, q % 2, :], f_buf[:, 0, q % 2, :], f_buf[:, 1, q % 2, :],
                                          ALU.add).then_inc(ssp_sum, 1)

                    terms_sum(0)
                    for q in range(4):
                        n = dve.snap(g * 4 + q)
                        us = range(QUAD * q, QUAD * (q + 1))
                        quad = slice(QUAD * q, QUAD * (q + 1))
                        dve.wait_ge(src_in[q], g * 16 + 16)
                        dve.wait_ge(mm_done, base + QUAD * (q + 1))
                        for u in us:
                            j = u % QUAD
                            i = dve.tensor_scalar(same[:, u, :], src_row[:, q, j * P:(j + 1) * P], rw_st[:, 0, u:u + 1],
                                                  None, ALU.is_equal)
                            i.then_inc(hot_ready, 1)
                        dve.wait_ge(hot_ready, base + QUAD * (q + 1))
                        for u in us:
                            i = dve.tensor_tensor_reduce(out=junk[:, u % QUAD, :], in0=same[:, u, :], in1=lower[:], scale=1.0,
                                                         scalar=0.0, op0=ALU.mult, op1=ALU.add, accum_out=dup[:, 0, u:u + 1])
                        i.then_inc(same_ready, 1)
                        dve.tensor_scalar(dup[:, 1, quad], rw_st[:, 0, quad], -1.0, dump[:], ALU.mult, ALU.add
                                          ).then_inc(dup_step, 1)
                        dve.wait_ge(same_ready, n + 5)
                        dve.tensor_scalar(dup[:, 0, quad], dup[:, 0, quad], 1.0, None, ALU.min).then_inc(dup_step, 1)
                        dve.wait_ge(dup_step, n * 3 + 2)
                        dve.tensor_tensor(dup[:, 2, quad], dup[:, 0, quad], dup[:, 1, quad], ALU.mult).then_inc(dup_step, 1)
                        dve.wait_ge(dup_step, n * 3 + 3)
                        dve.wait_ge(sums_free, g * 16 + 4 * q)
                        settle(dve)
                        dve.tensor_tensor(sum_row[:, quad], rw_st[:, 0, quad], dup[:, 2, quad], ALU.add
                                          ).then_inc(dest_ready, 1)
                        if q + 1 < 4:
                            terms_sum(q + 1)
                        dve.wait_ge(filt_mm, n + 1)
                        dve.wait_ge(row_in[q], reps * (5 * ngroups * 64) + g * 64 + 64)
                        for u in us:
                            j = u % QUAD
                            i = dve.scalar_tensor_tensor(out=msg[:, u, :], in0=ps[6 + q % 2][:, j * P:(j + 1) * P],
                                                         scalar=rw_st[:, 1, u:u + 1], in1=rows[:, u, :],
                                                         op0=ALU.mult, op1=ALU.mult)
                        i.then_inc(msg_ready, 1)

            run_pass(0)
            dve.wait_ge(add_done, reps * ntiles + GROUP)
            step(dve.tensor_scalar(counts, counts, 1.0, None, ALU.max))
            dve.reciprocal(counts, counts).then_inc(inv_ready, 1)
            dve.memset(rel_hot[:, :, NREL:NCNT], 0.0)
            for k, p in enumerate(DENSE):
                nck = n_chunks(p)
                if p["src"] == "bn":
                    dve.wait_ge(add_done, tiles_before(reps, k + 1) + GROUP)
                    step(dve.tensor_scalar(acc[:, 0:n_nodes], acc[:, 0:n_nodes], 0.0, None, ALU.max))
                    for c in range(n_nodes // bn_chunk):
                        last = dve.bn_stats(bn_st[:, c, :], acc[:, c * bn_chunk:(c + 1) * bn_chunk])
                    step(last)
                    step(dve.bn_aggr(bn[:, 0:2], bn_st[:]))
                    dve.tensor_scalar(bn[:, 2:3], bn[:, 1:2], EPS, None, ALU.add).then_inc(bn_var, 1)
                    dve.wait_ge(bn_sd, 1)
                    step(dve.reciprocal(bn[:, 4:5], bn[:, 3:4]))
                    step(dve.tensor_tensor(bn[:, 5:6], bn[:, 4:5], col["gamma"], ALU.mult))
                    step(dve.tensor_tensor(bn[:, 7:8], bn[:, 0:1], bn[:, 5:6], ALU.mult))
                    dve.tensor_tensor(bn[:, 6:7], col["beta"], bn[:, 7:8], ALU.subtract).then_inc(bn_ready, 1)
                with dve.Fori(0, nsb) as i:
                    if p["src"] == "sum":
                        dve.wait_ge(agg_read, i * 64 + 64)
                        for n, (a, b) in enumerate(((0, 1), (2, 3), (0, 2))):
                            if n == 2:
                                dve.wait_ge(agg_step, i * 3 + 2)
                            dve.tensor_tensor(agg_in[:, a], agg_in[:, a], agg_in[:, b], ALU.add).then_inc(agg_step, 1)
                        dve.wait_ge(out_parts, i + 1)
                        dve.tensor_tensor(yT[:], hT_s[:], tab_s[:, 0, 0:SB], ALU.add).then_inc(y_sum, 1)
                    if has_x(p):
                        dve.wait_ge(x_in, i * 16 + 16 * (turns(k, has_x) + 1))
                        dve.wait_ge(x_out, i * (16 * has_xout(p)) + 16 * turns(k, has_xout))
                        if has_ln(p):
                            dve.wait_ge(h_ready, i + turns(k, has_ln))
                        if has_upd(p):
                            dve.wait_ge(upd_mm, i + (turns(k, has_upd) + 1))
                            dve.tensor_tensor(flat(xn), ps[0][:], flat(xs), ALU.add).then_inc(x_new, 1)
                        else:
                            dve.tensor_copy(flat(xn), flat(xs)).then_inc(x_new, 1)
                    if has_ln(p):
                        n = turns(k, has_ln)
                        dve.wait_ge(x_new, i + (turns(k, has_x) + 1))
                        for j in range(4):
                            dve.bn_stats(st[:, j, :], xn[:, j, :]).then_inc(st_ready, 1)
                        dve.wait_ge(st_ready, i * 4 + (4 * n + 4))
                        settle(dve)
                        for j in range(4):
                            dve.bn_aggr(mv[:, j, :], st[:, j, :]).then_inc(mv_ready, 1)
                        dve.wait_ge(mv_ready, i * 4 + (4 * n + 4))
                        dve.tensor_scalar(nrm[:, :, 0], mv[:, :, 1], EPS, None, ALU.add).then_inc(var_ready, 1)
                        dve.wait_ge(sd_ready, i + (n + 1))
                        dve.reciprocal(nrm[:, :, 2], nrm[:, :, 1]).then_inc(rstd_ready, 1)
                        dve.wait_ge(rstd_ready, i + (n + 1))
                        dve.scalar_tensor_tensor(out=nrm[:, :, 3], in0=mv[:, :, 0], scalar=-1.0, in1=nrm[:, :, 2],
                                                 op0=ALU.mult, op1=ALU.mult).then_inc(nrm_ready, 1)
                    for c in range(1, nck, 2):
                        j, cut = c // len(cuts(p)), cuts(p)[c % len(cuts(p))]
                        dve.wait_ge(tab_mm, i * nck + (chunks(k) + c + 1))
                        dve.wait_ge(tab_out[j % LANES], i * (16 * 4 // LANES) + 16 * (lane_uses(k) + j // LANES))
                        dve.tensor_copy(tab_s[:, j % LANES, cut[0]:cut[1]], ps[3 + c % 4][:, 0:cut[1] - cut[0]]
                                        ).then_inc(evac_v, 1)
                if k == 2:
                    dve.wait_ge(late_in, 32)
                    dve.scalar_tensor_tensor(out=row_i[:, 0:ntiles], in0=src_i[:], scalar=3.0, in1=etype[:, :].bitcast(I32),
                                             op0=ALU.mult, op1=ALU.add).then_inc(rows_ready, 1)
                if k == 3:
                    dve.tensor_copy(row_i[:, 0:ntiles], src_i[:]).then_inc(rows_ready, 1)
                if k == 5:
                    dve.tensor_copy(row_i[:, 0:ntiles], dst_i[:]).then_inc(rows_ready, 1)
                    for j in range(LANES):
                        dve.wait_ge(tab_out[j], 16 * lane_uses(k + 1))
                    filter_pass()
                elif has_table(p):
                    if has_root(p):
                        dve.wait_ge(acc_init, turns(k + 1, has_root))
                    else:
                        dve.wait_ge(y_ready, turns(k + 1, has_src))
                        dve.memset(acc[:], 0.0)
                    for j in range(LANES):
                        dve.wait_ge(tab_out[j], 16 * lane_uses(k + 1))
                    run_pass(k + 1)


def kernel(**inputs):
    import concourse.bacc as bacc
    from concourse.bass_utils import run_bass_kernel_spmd

    a = {n: np.asarray(v) for n, v in inputs.items()}
    n_nodes, n_edges = a["x"].shape[0], a["src"].shape[0]
    nacc = -(-(n_nodes + P) // SB) * SB
    ntiles = -(-n_edges // (GROUP * P)) * GROUP
    pad = ntiles * P - n_edges

    def per_edge(v, fill):
        return np.concatenate([v, np.full(pad, fill, v.dtype)]).reshape(ntiles, P).T

    dst = per_edge(a["dst"], n_nodes)
    attr = np.concatenate([a["edge_attr_42"][:, 16:26], np.zeros((pad, 10), np.float32)])
    feat = np.concatenate([a["edge_attr_20"], np.zeros((pad, 20), np.float32)])
    rel = lambda w: w.transpose(1, 0, 2).reshape(w.shape[1], -1)
    vectors = ["L0_gnn_b1", "L0_gnn_b2", "L2_gnn_bl1", "L2_gnn_bl2", "L2_gnn_gamma", "L2_gnn_beta",
               "L3_gnn_b_filt1", "L3_gnn_b_out1"]
    laid = dict(
        x=np.concatenate([a["x"], np.zeros((nacc - n_nodes, a["x"].shape[1]), np.float32)]),
        src=per_edge(a["src"], 0), src_row=np.concatenate([a["src"], np.zeros(pad, np.int32)])[None], dst=dst, first=np.broadcast_to(dst[0:1, :], dst.shape),
        type=per_edge(a["edge_type_3"], 0), weight=per_edge(a["edge_weight"], 0),
        attr=attr.reshape(ntiles, P, 10).transpose(1, 0, 2), feat=feat.T,
        wrel=rel(a["L0_gnn_w_rel1"]), wrel2=rel(a["L0_gnn_w_rel2"]), root1=a["L0_gnn_root1"], root2=a["L0_gnn_root2"],
        w1=rel(a["L1_gnn_weight"]), wl1=a["L2_gnn_Wl1"].T, wr1=a["L2_gnn_Wr1"].T, wl2=a["L2_gnn_Wl2"].T,
        wr2=a["L2_gnn_Wr2"].T, fcw=a["L2_gnn_fcW"].T, win=a["L3_gnn_W_in2f"], wout1=a["L3_gnn_W_out1"],
        wout2=a["L3_gnn_W_out2"], wfilt2=a["L3_gnn_W_filt2"], wfilt1=a["L3_gnn_W_filt1"],
        cols=np.stack([a[v] for v in vectors], 1), fcb=a["L2_gnn_fcb"][None], bout2=a["L3_gnn_b_out2"][None],
        bfilt2=a["L3_gnn_b_filt2"][None])

    nc = bacc.Bacc("TRN2", target_bir_lowering=False, num_devices=1)
    arrays, handles = {}, {}
    for name, v in laid.items():
        arrays[f"in_{name}"] = v = np.ascontiguousarray(v)
        handles[name] = nc.dram_tensor(f"in_{name}", v.shape, mybir.dt.from_np(v.dtype), kind="ExternalInput").ap()
    out = nc.dram_tensor("out_x", (nacc, P), F32, kind="ExternalOutput").ap()
    build(nc, handles, out, n_nodes, n_edges)
    got = run_bass_kernel_spmd(nc, [arrays], core_ids=[0])
    return got.results[0]["out_x"][:n_nodes]
```

```python
from contextlib import ExitStack

import numpy as np
import concourse.bass as bass
from concourse import mybir

F32 = mybir.dt.float32
BF16 = mybir.dt.bfloat16
I32 = mybir.dt.int32
ALU = mybir.AluOpType
ACT = mybir.ActivationFunctionType
AX = mybir.AxisListType
ENG = mybir.EngineType

P = 128
GROUP = 16
QUAD = 4
SB = 4 * P
EPS = 1e-5
BANK = 512
LANES = 2
AHEAD = 2
COPIES = QUAD

DENSE = [
    dict(src="", upd="", ln=True, table="wrel", rels=10, root="root1", bias="b1_0", xin=0, xout=None),
    dict(src="relu", upd="", ln=False, table="wrel", rels=10, root="root2", bias="b1_1", xin=None, xout=None),
    dict(src="copy", upd="ident", ln=True, table="w1", rels=3, root="", xin=0, xout=1),
    dict(src="relu", upd="ident", ln=True, table="wl1", rels=1, root="wr1", bias="bl1", xin=1, xout=2),
    dict(src="relu", upd="", ln=False, table="wl2", rels=1, root="wr2", bias="bl2", xin=None, xout=None),
    dict(src="bn", upd="fcw", row="fcb", ln=True, table="win", rels=1, root="", xin=2, xout=3),
    dict(src="sum", upd="wout2", row="bout2", ln=False, table="", rels=0, root="", xin=3, xout=4),
]
NREL = 10
NCNT = NREL + 1
PART = 32
COUNT, LOOKUP, PLAIN, FILTER = range(4)
PASSES = [COUNT, LOOKUP, PLAIN, PLAIN, PLAIN, PLAIN, FILTER]
COLS = ["b1_0", "b1_1", "bl1", "bl2", "gamma", "beta", "bfilt1", "bout1"]
WEIGHTS = [("wrel", NREL * P), ("root1", P), ("root2", P), ("w1", 3 * P), ("wl1", P), ("wr1", P), ("wl2", P),
           ("wr2", P), ("fcw", P), ("win", P), ("wout1", P), ("wout2", P), ("wfilt2", P)]
ROWS = ["fcb", "bout2", "bfilt2"]


def build(nc, d, out, n_nodes, n_edges):
    nsb = -(-(n_nodes + P) // SB)
    nacc = nsb * SB
    ngroups = -(-n_edges // (GROUP * P))
    ntiles = ngroups * GROUP
    nwin = -(-n_nodes // P)
    bn_chunk = max(c for c in range(1, BANK + 1) if n_nodes % c == 0)
    n_feat = 20

    def turns(k, flag):
        return nsb * sum(bool(flag(p)) for p in DENSE[:k])

    def has_src(p): return p["src"] != ""
    def has_x(p): return p["xin"] is not None
    def has_xout(p): return p["xout"] is not None
    def has_upd(p): return p["upd"] != ""
    def has_ln(p): return p["ln"]
    def has_root(p): return p["root"] != ""
    def has_table(p): return p["rels"] > 0

    def cuts(p):
        return [(a, min(a + BANK, p["rels"] * P)) for a in range(0, p["rels"] * P, BANK)]

    def n_chunks(p):
        return 4 * len(cuts(p))

    nq = 4 * ngroups + AHEAD

    def chunks(k):
        return nsb * sum(n_chunks(p) for p in DENSE[:k])

    with ExitStack() as ctx:
        def sb(name, shape, dt=F32):
            return ctx.enter_context(nc.sbuf_tensor(name, shape, dt))

        def sem(name):
            return ctx.enter_context(nc.semaphore(name))

        x_dram = [d["x"]] + [nc.dram_tensor(f"x{k}_dram", (nacc, P), F32).ap() for k in (1, 2, 3)] + [out]
        x_dram = [x.rearrange("(s j p) c -> p s j c", j=4, p=P) for x in x_dram]
        table_dram = {r: nc.dram_tensor(f"table{r}_dram", (nacc * r, P), F32).ap() for r in (NREL, 3, 1)}

        agg_dram = [nc.dram_tensor(f"agg{c}_dram", (nacc + P, P), F32).ap() for c in range(COPIES)]

        spread = NCNT * nacc // P
        counts_dram = nc.dram_tensor("counts_dram", (NCNT, nacc), F32).ap()
        parts_dram = [nc.dram_tensor(f"part{k}_dram", (NCNT, nacc), BF16).ap() for k in range(3)]
        over_all = lambda t: t.rearrange("r n -> (r n)").rearrange("(p w) -> p w", p=P)

        acc = sb("acc", [P, max(nacc, 2 * P * NREL, GROUP * P + 2 * BANK)])
        scratch = sb("scratch", [P, max(nacc, 3 * GROUP * P + 8 * BANK + 2 * P, 2 * COPIES * SB)])
        src_i = sb("src_i", [P, ntiles], I32)
        row_i = sb("row_i", [P, ntiles], I32)
        dst_i = sb("dst_i", [P, ntiles], I32)
        first_i = sb("first_i", [P, ntiles], I32)
        rel_dst = sb("rel_dst", [P, ntiles])
        win_i = sb("win_i", [1, ntiles // QUAD], I32)
        etype = sb("etype", [P, ntiles])
        wt_a = sb("wt_a", [P, ntiles])
        wt_deg = sb("wt_deg", [P, ntiles])
        ident = sb("ident", [P, P])
        ident_b = sb("ident_b", [P, P], BF16)
        iota_i = sb("iota_i", [P, P], I32)
        iota = sb("iota", [P, P])
        ones = sb("ones", [P, P])
        iota_b = sb("iota_b", [P, P], BF16)
        sel_deg = sb("sel_deg", [P, P], BF16)
        W = {n: sb(n, [P, w]) for n, w in WEIGHTS}
        W["ident"] = ident
        wfilt1 = sb("wfilt1", [n_feat, P])
        bias_row = {n: sb(n, [1, P]) for n in ROWS}
        bfilt2_quad = sb("bfilt2_quad", [3 * PART, BANK], BF16)
        bias_rest = sb("bias_rest", [1, P])
        part_b = sb("part_b", [1, P], BF16)
        ones_b = sb("ones_b", [3 * PART, P], BF16)
        cols = sb("cols", [P, len(COLS)])
        col = {n: cols[:, i:i + 1] for i, n in enumerate(COLS)}
        half = sb("half", [P, 1])
        zeros = sb("zeros", [P, P])
        lower = sb("lower", [P, P])
        dump = sb("dump", [P, 1])
        place = sb("place", [P, 1])
        dump_i = sb("dump_i", [P, 1], I32)
        src_st = sb("src_st", [P, GROUP])
        dup = sb("dup", [P, 3, GROUP])
        sum_row = sb("sum_row", [P, GROUP], I32)
        reps_f = sb("reps_f", [P, 6])
        reps_i = sb("reps_i", [P, 1], I32)
        general, fast = reps_f[:, 4:5], reps_f[:, 5:6]
        win0 = sb("win0", [P, 2])
        bn = sb("bn", [P, 8])
        bn_st = sb("bn_st", [P, n_nodes // bn_chunk, 6])

        xs = sb("xs", [P, 4, P])
        yT = sb("yT", [P, SB])
        xn_h = sb("xn_h", [P, 2, 4, P])
        xn, h = xn_h[:, 0], xn_h[:, 1]
        hT_s = sb("hT_s", [P, SB])
        tab_s = sb("tab_s", [P, LANES, NREL * P])
        st = sb("st", [P, 4, 6])
        mv = sb("mv", [P, 4, 2])
        nrm = sb("nrm", [P, 4, 4])
        flat = lambda t: t[:, :, :].rearrange("p j c -> p (j c)")

        rows = sb("rows", [P, GROUP, P])
        hot = flat(tab_s)[:, 0:GROUP * P].rearrange("p (u n) -> p u n", u=GROUP)
        picked = flat(rows)[:, 0:2 * BANK].rearrange("p (b e) -> p b e", b=2)
        row_st = sb("row_st", [P, GROUP], I32)
        rw_st = sb("rw_st", [P, 2, GROUP])
        wout_st = sb("wout_st", [P, 2, GROUP])
        rel_hot = sb("rel_hot", [P, GROUP, NCNT], BF16)
        rev = sb("rev", [P, NREL])
        junk = xs
        hot_b = flat(tab_s).bitcast(BF16)[:, 0:GROUP * P].rearrange("p (u n) -> p u n", u=GROUP)
        rel_hot3 = xn_h[:, :, :, :].rearrange("p a j c -> p (a j c)").bitcast(BF16).rearrange(
            "p (u k) -> p u k", u=GROUP)
        rel_hotT = yT[:, :].bitcast(BF16).rearrange("p (b e) -> p b e", b=2)
        counts = scratch[0:NCNT, 0:nacc]
        wide = scratch[:, nacc // 2:nacc // 2 + spread]
        wide_part = [scratch[:, nacc // 2 + spread:nacc].bitcast(BF16)[:, k * spread:(k + 1) * spread] for k in range(3)]
        inv3 = scratch[:, :].bitcast(BF16)[:, 0:nacc]
        msg = scratch[:, 0:GROUP * P].rearrange("p (u c) -> p u c", u=GROUP)
        dest = etype[:, :].bitcast(I32)
        pairs, pairs_junk = xn, h
        same = hot
        src_row = scratch[:, 2 * GROUP * P + 6 * BANK:3 * GROUP * P + 6 * BANK].bitcast(I32).rearrange(
            "p (q e) -> p q e", q=4)
        dst_row = scratch[:, 3 * GROUP * P + 6 * BANK:3 * GROUP * P + 8 * BANK].bitcast(I32).rearrange(
            "p (b e) -> p b e", b=2)
        nodes = scratch[:, 3 * GROUP * P + 8 * BANK:3 * GROUP * P + 8 * BANK + 2 * P].rearrange(
            "p (b c) -> p b c", b=2)
        hotT = acc[:, GROUP * P:GROUP * P + 2 * BANK].rearrange("p (b e) -> p b e", b=2)
        node_id = wt_deg[:, 0:ntiles // QUAD]
        node_st = sb("node_st", [P, QUAD])
        sums = acc[:, 0:GROUP * P].rearrange("p (q b) -> p q b", q=4)
        agg_in = scratch[:, 0:2 * COPIES * SB].rearrange("p (b k j c) -> p b k j c", b=2, k=COPIES, j=4)
        feat = scratch[0:n_feat, GROUP * P:2 * GROUP * P].rearrange("p (q e) -> p q e", q=4)
        f_buf = scratch[:, 2 * GROUP * P:2 * GROUP * P + 6 * BANK].rearrange("p (k b e) -> p k b e", k=3, b=2)
        attr = acc[:, 0:2 * P * NREL].rearrange("p (b t r) -> p b t r", b=2, r=NREL)

        ps = [ctx.enter_context(nc.psum_tensor(f"ps{k}", [P, BANK], F32)) for k in range(8)]

        loaded = sem("loaded")
        attr_in = [sem("attr_in0"), sem("attr_in1")]
        attr_used = sem("attr_used")
        made = sem("made")
        prep = sem("prep")
        bad_ready = sem("bad_ready")
        bad_sum = sem("bad_sum")
        reps_ready = sem("reps_ready")
        late_in = sem("late_in")
        wrel2_in = sem("wrel2_in")
        rows_ready = sem("rows_ready")
        win_ready = sem("win_ready")
        win_step = sem("win_step")
        src_staged = sem("src_staged")
        row_staged = sem("row_staged")
        row_in = [sem(f"row_in{q}") for q in range(4)]
        rw_staged = sem("rw_staged")
        hot_made = sem("hot_made")
        deg_step = sem("deg_step")
        deg_done = sem("deg_done")
        hot_ready = sem("hot_ready")
        mm_done = sem("mm_done")
        add_done = sem("add_done")
        rel_ready = sem("rel_ready")
        relT_mm = sem("relT_mm")
        relT_ready = sem("relT_ready")
        look_mm = sem("look_mm")
        counts_out = sem("counts_out")
        wide_in = sem("wide_in")
        parts_ready = sem("parts_ready")
        parts_out = sem("parts_out")
        inv_in = sem("inv_in")
        inv_ready = sem("inv_ready")
        feat_in = [sem(f"feat_in{q}") for q in range(4)]
        f1_mm = sem("f1_mm")
        ssp_step = sem("ssp_step")
        ssp_parts = sem("ssp_parts")
        ssp_sum = sem("ssp_sum")
        filt_mm = sem("filt_mm")
        msg_ready = sem("msg_ready")
        src_in = [sem(f"src_in{q}") for q in range(4)]
        dst_in = [sem("dst_in0"), sem("dst_in1")]
        nodes_in = [sem("nodes_in0"), sem("nodes_in1")]
        hotT_ready = sem("hotT_ready")
        pick_mm = sem("pick_mm")
        pick_ready = sem("pick_ready")
        same_ready = sem("same_ready")
        pair_step = sem("pair_step")
        dup_step = sem("dup_step")
        dest_ready = sem("dest_ready")
        scattered = [sem(f"scattered{j}") for j in range(COPIES)]
        sums_free = sem("sums_free")
        agg_read = [sem("agg_read0"), sem("agg_read1")]
        agg_step = sem("agg_step")
        aggT_mm = sem("aggT_mm")
        x_in = sem("x_in")
        y_copy = sem("y_copy")
        out_mm = sem("out_mm")
        out_parts = sem("out_parts")
        y_sum = sem("y_sum")
        y_ready = sem("y_ready")
        upd_mm = sem("upd_mm")
        x_new = sem("x_new")
        x_out = sem("x_out")
        st_ready = sem("st_ready")
        mv_ready = sem("mv_ready")
        rstd_ready = sem("rstd_ready")
        var_ready = sem("var_ready")
        sd_ready = sem("sd_ready")
        nrm_ready = sem("nrm_ready")
        h_ready = sem("h_ready")
        hT_mm = sem("hT_mm")
        hT_ready = sem("hT_ready")
        root_mm = sem("root_mm")
        acc_init = sem("acc_init")
        tab_mm = sem("tab_mm")
        evac_a = sem("evac_a")
        evac_v = sem("evac_v")
        tab_out = [sem(f"tab_out{j}") for j in range(LANES)]
        bn_var = sem("bn_var")
        bn_sd = sem("bn_sd")
        bn_ready = sem("bn_ready")

        settled = sem("settled")

        n_loads = 3 + len(WEIGHTS) + 2 + len(ROWS)
        n_attr = -(-ntiles // P)

        def reps_of(e):
            e.wait_ge(reps_ready, 1)
            return e.value_load(reps_i[0:1, 0:1], min_val=1, max_val=nwin)

        def settle(e):
            e.sem_inc(settled, 1)

        def tiles_before(reps, pn):
            return reps * (pn * ntiles)

        def windows(e, g):
            return nc.values_load_multi_w_load_instructions(
                win_i[0:1, bass.ds(g * QUAD, QUAD)], engines=[e.engine], min_val=0, max_val=n_nodes,
                skip_runtime_bounds_check_because="a destination or the start of a window of nodes, from 0 to n_nodes")[1]

        def superblocks(e, p, body):
            if p["src"] == "sum":
                body(0, None, 0, 0)
                if nsb > 2:
                    with e.Fori(0, (nsb - 1) // 2) as i:
                        body(i * 2 + 1, i * 2, 1, i)
                        body(i * 2 + 2, i * 2 + 1, 0, i + 1)
                if nsb % 2 == 0:
                    body(nsb - 1, nsb - 2, 1, (nsb - 1) // 2)
                body(None, nsb - 1, 0, 0)
                return
            if not has_ln(p):
                with e.Fori(0, nsb) as i:
                    body(i, i)
                return
            body(0, None)
            with e.Fori(0, nsb - 1) as i:
                body(i + 1, i)
            body(None, nsb - 1)

        def is_wide(p):
            return 4 * p["rels"] * P > LANES * NREL * P

        def lane(p, j):
            return j % LANES if is_wide(p) else 0

        def staged(p, j, a, b):
            if is_wide(p):
                return tab_s[:, lane(p, j), a:b]
            return flat(tab_s)[:, j * p["rels"] * P + a:j * p["rels"] * P + b]

        def lane_uses(k, v):
            return 1 + nsb * sum((4 // LANES if is_wide(p) else v == 0) for p in DENSE[:k] if has_table(p))

        def wait_lane(e, k, i, j):
            v = lane(DENSE[k], j)
            if is_wide(DENSE[k]):
                e.wait_ge(tab_out[v], i * (16 * 4 // LANES) + 16 * (lane_uses(k, v) + j // LANES))
            else:
                e.wait_ge(tab_out[v], i * 16 + 16 * lane_uses(k, v))

        def wait_stores(e, k):
            for v in range(LANES):
                e.wait_ge(tab_out[v], 16 * lane_uses(k + 1, v))

        block = ctx.enter_context(nc.Block())

        @block.sync
        def _(sp):
            for dst, name in ([(src_i, "src"), (dst_i, "dst"), (first_i, "first")] + [(W[n], n) for n, _ in WEIGHTS]
                              + [(wfilt1, "wfilt1"), (cols, "cols")] + [(bias_row[n], n) for n in ROWS]):
                sp.dma_start(dst[:], d[name]).then_inc(loaded, 16)
            for c in range(n_attr):
                n = min(P, ntiles - c * P)
                if c >= 2:
                    sp.wait_ge(attr_used, c - 1)
                sp.dma_start(attr[:, c % 2, 0:n, :], d["attr"][:, c * P:c * P + n, :]).then_inc(attr_in[c % 2], 16)
            reps = reps_of(sp)
            sp.wait_ge(add_done, reps * ntiles + GROUP)
            settle(sp)
            sp.dma_start(counts_dram, counts).then_inc(counts_out, 16)
            sp.wait_ge(counts_out, 16)
            sp.dma_start(wide, over_all(counts_dram)).then_inc(wide_in, 16)
            sp.wait_ge(parts_ready, 1)
            for k in range(3):
                sp.dma_start(over_all(parts_dram[k]), wide_part[k]).then_inc(parts_out, 16)
            sp.wait_ge(parts_out, 48)
            for k in range(3):
                sp.dma_start(inv3[(k + 1) * PART:(k + 1) * PART + NCNT, :], parts_dram[k]).then_inc(inv_in, 16)

            for k, p in enumerate(DENSE):
                if has_x(p):
                    sp.wait_ge(x_out, 16 * turns(k, has_xout))

                    def load_sums(i, b):
                        sp.wait_ge(aggT_mm, i + 1)
                        settle(sp)
                        for c in range(COPIES):
                            sp.dma_start(agg_in[:, b, c, :, :], agg_dram[c][0:nacc, :].rearrange(
                                "(s j p) c -> p s j c", j=4, p=P)[:, bass.ds(i, 1)].rearrange("p s j c -> p (s j) c")
                            ).then_inc(agg_read[b], 16)

                    def move_x(i):
                        sp.wait_ge(x_new, i + (turns(k, has_x) + 1))
                        sp.dma_start(xs[:], x_dram[p["xin"]][:, bass.ds(i, 1)].rearrange("p s j c -> p (s j) c")
                                     ).then_inc(x_in, 16)
                        if has_xout(p):
                            sp.wait_ge(x_new, i + (turns(k, has_x) + 2))
                            sp.dma_start(x_dram[p["xout"]][:, bass.ds(i, 1)].rearrange("p s j c -> p (s j) c"), xn[:]
                                         ).then_inc(x_out, 16)

                    if p["src"] == "sum":
                        load_sums(0, 0)
                        load_sums(1, 1)
                        pairs = (nsb - 2) // 2
                        if pairs:
                            with sp.Fori(0, pairs) as i:
                                for b in range(2):
                                    load_sums(i * 2 + (b + 2), b)
                                    move_x(i * 2 + b)
                        for i in range(2 * pairs, nsb):
                            if i + 2 < nsb:
                                load_sums(i + 2, i % 2)
                            move_x(i)
                    else:
                        with sp.Fori(0, nsb) as i:
                            move_x(i)
                if k == 0:
                    sp.wait_ge(tab_mm, chunks(1) + 1)
                    sp.dma_start(W["wrel"][:], d["wrel2"]).then_inc(wrel2_in, 16)
                if k == 1:
                    sp.wait_ge(add_done, reps * (3 * ntiles) + GROUP)
                    sp.dma_start(etype[:, :].bitcast(I32), d["type"]).then_inc(late_in, 16)
                    sp.dma_start(wt_a[:], d["weight"]).then_inc(late_in, 16)
                def load_sources(before, g, q):
                    sp.wait_ge(same_ready, before + 1)
                    sp.dma_start(src_row[:, q, :], d["src_row"][0:1, bass.ds(g * (GROUP * P) + q * BANK, BANK)
                                                                ].broadcast_to([P, BANK])).then_inc(src_in[q], 16)

                if k == 4:
                    sp.wait_ge(add_done, tiles_before(reps, 5) + GROUP)
                    settle(sp)
                    with sp.Fori(0, reps) as r:
                        with sp.Fori(0, ngroups) as g:
                            for q in range(4):
                                load_sources((r * ngroups + g) * 4 + q, g, q)
                if k == 5:
                    sp.wait_ge(add_done, tiles_before(reps, 6) + GROUP)
                    for v in range(LANES):
                        sp.wait_ge(tab_out[v], 16 * lane_uses(k + 1, v))
                    settle(sp)

                    def load_features(r, q, before, edges):
                        sp.wait_ge(f1_mm, r * nq + before + (q + 3))
                        sp.dma_start(feat[:, q, :], d["feat"][:, edges]).then_inc(feat_in[q], 16)

                    with sp.Fori(0, reps) as r:
                        sp.wait_ge(win_ready, reps * 6 + r + 1)
                        settle(sp)
                        with sp.Fori(0, ngroups) as g:
                            win = windows(sp, g)
                            n0 = sp.snap((r * ngroups + g) * 4)
                            for q in range(4):
                                edges = bass.ds(g * (GROUP * P) + q * BANK, BANK)
                                load_features(r, q, g * 4, edges)
                                sp.wait_ge(hotT_ready, n0 + (q + 1))
                                sp.dma_start(dst_row[:, q % 2, :], d["dst_row"][0:1, edges].broadcast_to([P, BANK])
                                             ).then_inc(dst_in[q % 2], 16)
                                sp.wait_ge(pick_mm, n0 + (q + 1))
                                settle(sp)
                                sp.dma_start(nodes[:, q % 2, :], table_dram[1][bass.ds(win[q], P), :]
                                             ).then_inc(nodes_in[q % 2], 16)
                                load_sources(reps * (4 * ngroups) + n0 + q, g, q)
                        for q in range(AHEAD):
                            load_features(r, q, 4 * ngroups, slice(ntiles * P + q * BANK, ntiles * P + (q + 1) * BANK))
                    for s in scattered:
                        sp.wait_ge(s, reps * (64 * ngroups) + 16)
                    settle(sp)
            sp.wait_ge(x_out, 16 * turns(len(DENSE), has_xout))

        @block.gpsimd
        def _(pool):
            pool.memset(ident[:], 0.0).then_inc(made, 1)
            pool.memset(sel_deg[:], 0.0).then_inc(made, 1)
            pool.memset(ones[:], 1.0).then_inc(made, 1)
            pool.memset(half[:], 0.5).then_inc(made, 1)
            pool.iota(iota_i[:], pattern=[[1, P]], base=0, channel_multiplier=0).then_inc(made, 1)
            pool.memset(zeros[:], 0.0).then_inc(made, 1)
            pool.memset(lower[:], 0.0).then_inc(made, 1)
            pool.iota(dump_i[:], pattern=[[0, 1]], base=nacc, channel_multiplier=1).then_inc(made, 1)
            pool.wait_ge(made, 8)
            pool.affine_select(out=ident[:], in_=ident[:], compare_op=ALU.not_equal, fill=1.0, base=0,
                               pattern=[[-1, P]], channel_multiplier=1).then_inc(made, 1)
            for k in (1, 2, 3):
                pool.affine_select(out=sel_deg[:], in_=sel_deg[:], compare_op=ALU.not_equal, fill=1.0, base=-(k * PART + NREL),
                                   pattern=[[0, P]], channel_multiplier=1).then_inc(made, 1)
                pool.wait_ge(made, 9 + k)
            pool.affine_select(out=lower[:], in_=lower[:], compare_op=ALU.is_ge, fill=1.0, base=0,
                               pattern=[[1, P]], channel_multiplier=-1).then_inc(made, 1)
            pool.sem_inc(sums_free, 3 * QUAD)
            for c, (agg, s) in enumerate(zip(agg_dram, scattered)):
                blocks = nsb * 4 + (c >= LANES)
                pool.dma_start(agg[0:blocks * P].rearrange("(r p) c -> p r c", p=P),
                               zeros[:, :].unsqueeze(1).broadcast_to([P, blocks, P])).then_inc(s, 16)
                if c < LANES:
                    pool.dma_start(agg[blocks * P:(blocks + 1) * P], zeros[:]).then_inc(tab_out[c], 16)
            reps = reps_of(pool)

            for k, p in enumerate(DENSE):
                if not has_table(p):
                    continue
                width = p["rels"] * P
                table = table_dram[p["rels"]].rearrange("(s j p r) c -> p s j (r c)", j=4, p=P, r=p["rels"])
                with pool.Fori(0, nsb) as i:
                    for j in range(4):
                        if not is_wide(p) and j < 3:
                            continue
                        done = (j + 1) * len(cuts(p))
                        pool.wait_ge(evac_a, i * (n_chunks(p) // 2) + (2 + chunks(k) // 2 + (done + 1) // 2))
                        pool.wait_ge(evac_v, i * (n_chunks(p) // 2) + (2 + chunks(k) // 2 + done // 2))
                        if is_wide(p):
                            pool.dma_start(table[:, bass.ds(i, 1), j, :].rearrange("p s w -> p (s w)"),
                                           staged(p, j, 0, width)).then_inc(tab_out[lane(p, j)], 16)
                        else:
                            pool.dma_start(table[:, bass.ds(i, 1), :, :].rearrange("p s j w -> p (s j) w"),
                                           flat(tab_s)[:, 0:4 * width].rearrange("p (j w) -> p j w", j=4)
                                           ).then_inc(tab_out[0], 16)
                wait_stores(pool, k)
                if PASSES[k + 1] != FILTER:
                    pool.wait_ge(rows_ready, sum(q in (0, 2, 3) for q in range(k + 1)))
                else:
                    with pool.Fori(0, reps) as r:
                        with pool.Fori(0, ngroups) as g:
                            n0 = pool.snap((r * ngroups + g) * 4)
                            base = pool.snap(tiles_before(reps, 6) + n0 * QUAD)
                            for q in range(4):
                                pool.wait_ge(dest_ready, n0 + (q + 2))
                                pool.wait_ge(add_done, base + (GROUP + QUAD * (q + 1)))
                                for j in range(QUAD):
                                    pool.wait_ge(scattered[j], n0 * 16 + 16 * (q + 1))
                                    pool.sem_inc(sums_free, 1)
                                    pool.indirect_dma_start(
                                        agg_dram[j],
                                        bass.IndirectOffsetOnAxis(ap=sum_row[:, QUAD * q + j:QUAD * q + j + 1], axis=0),
                                        sums[:, q, j * P:(j + 1) * P], None, compute_op=ALU.add).then_inc(scattered[j], 16)
                    continue
                with pool.Fori(0, reps) as r:
                    with pool.Fori(0, ngroups) as g:
                        turn = pool.snap(reps * (k * ngroups) + r * ngroups + g)
                        used = pool.snap(reps * ntiles + turn * GROUP)
                        for part in range(2):
                            pool.wait_ge(mm_done, used + (part + 1) * (GROUP // 2))
                            us = range(part * (GROUP // 2), (part + 1) * (GROUP // 2))
                            pool.tensor_copy(row_st[:, us[0]:us[-1] + 1],
                                             row_i[:, bass.ds(g * GROUP + us[0], GROUP // 2)]).then_inc(row_staged, 1)
                            pool.wait_ge(row_staged, turn * 2 + (part + 1))
                            settle(pool)
                            for u in us:
                                pool.indirect_dma_start(
                                    rows[:, u, :], None, table_dram[p["rels"]],
                                    bass.IndirectOffsetOnAxis(ap=row_st[:, u:u + 1], axis=0)
                                ).then_inc(row_in[u // QUAD], 16)

        @block.scalar
        def _(act):
            act.sem_inc(evac_a, 2)
            for s in (relT_ready, y_copy, out_parts, pick_ready, ssp_parts, hT_ready, acc_init):
                act.sem_inc(s, 1)
            reps = reps_of(act)

            def softplus_terms(src, bias, a, b, sig, before):
                act.activation(a, src, ACT.Abs, bias=bias).then_inc(ssp_step, 1)
                act.activation(b, src, ACT.Relu, bias=bias)
                act.wait_ge(ssp_step, before + 1)
                act.activation(a, a, ACT.Exp, scale=-1.0).then_inc(ssp_step, 1)
                act.wait_ge(ssp_step, before + 2)
                act.activation(a, a, ACT.Ln, bias=half[:], scale=0.5).then_inc(sig, 1)

            for k, p in enumerate(DENSE):
                nck = n_chunks(p)
                hT = hT_s if has_ln(p) else yT
                act.wait_ge(add_done, tiles_before(reps, k + 1) + GROUP)
                if p["src"] == "bn":
                    act.wait_ge(bn_var, 1)
                    act.activation(bn[:, 3:4], bn[:, 2:3], ACT.Sqrt).then_inc(bn_sd, 1)
                    act.wait_ge(bn_ready, 1)
                if p["src"] == "sum":
                    settle(act)
                    nc.scalar.preload_act_table_set("natural_log_exp_and_others")

                def body(f, l, b=0, uses=0):
                    if f is not None:
                        acc_f = acc[:, bass.ds(f * SB, SB)]
                        if has_upd(p) and p["src"] != "sum":
                            act.wait_ge(upd_mm, f + turns(k, has_upd))
                        elif has_src(p) and p["src"] != "sum":
                            act.wait_ge(tab_mm, f * nck + (chunks(k) + 1))
                        settle(act)
                        if p["src"] == "copy":
                            act.activation(yT[:], acc_f, ACT.Copy).then_inc(y_ready, 1)
                        elif p["src"] == "relu":
                            act.activation(yT[:], acc_f, ACT.Relu).then_inc(y_ready, 1)
                        elif p["src"] == "bn":
                            act.activation(yT[:], acc_f, ACT.Identity, bias=bn[:, 6:7], scale=bn[:, 5:6]).then_inc(y_ready, 1)
                        elif p["src"] == "sum":
                            act.wait_ge(aggT_mm, f + 3)
                            act.wait_ge(out_mm, f + 1)
                            act.activation(flat(h), ps[1][:], ACT.Copy).then_inc(y_copy, 1)
                            act.wait_ge(out_mm, f + 2)
                            act.wait_ge(y_sum, f + 1)
                            softplus_terms(ps[7][:], col["bout1"], hT_s[:], tab_s[:, 0, 0:SB], out_parts,
                                           f * 2 + reps * (2 * nq))
                    if l is not None and has_ln(p):
                        act.wait_ge(hT_mm, l + (turns(k, has_ln) + 1))
                        act.wait_ge(tab_mm, l * nck + (chunks(k) + 1))
                        act.activation(hT_s[:], ps[1][:], ACT.Copy).then_inc(hT_ready, 1)
                    if f is not None and has_ln(p):
                        n = turns(k, has_ln)
                        act.wait_ge(var_ready, f + (n + 1))
                        act.activation(nrm[:, :, 1], nrm[:, :, 0], ACT.Sqrt).then_inc(sd_ready, 1)
                    if l is not None and has_root(p):
                        act.wait_ge(root_mm, l + (turns(k, has_root) + 1))
                        settle(act)
                        act.activation(acc[:, bass.ds(l * SB, SB)], ps[2][:], ACT.Identity, bias=col[p["bias"]]
                                       ).then_inc(acc_init, 1)
                    if f is not None and has_ln(p):
                        act.wait_ge(nrm_ready, f + (n + 1))
                        act.wait_ge(hT_mm, f + n)
                        for j in range(4):
                            a = act.activation(h[:, j, :], xn[:, j, :], ACT.Relu, bias=nrm[:, j, 3:4], scale=nrm[:, j, 2:3])
                        a.then_inc(h_ready, 1)
                    if l is not None and has_table(p):
                        for c in range(0, nck, 2):
                            j, cut = c // len(cuts(p)), cuts(p)[c % len(cuts(p))]
                            act.wait_ge(tab_mm, l * nck + (chunks(k) + c + 2))
                            wait_lane(act, k, l, j)
                            act.activation(staged(p, j, *cut), ps[3 + c % 4][:, 0:cut[1] - cut[0]],
                                           ACT.Copy).then_inc(evac_a, 1)

                superblocks(act, p, body)
                if k + 1 < len(PASSES) and PASSES[k + 1] == LOOKUP:
                    with act.Fori(0, reps) as r:
                        with act.Fori(0, ngroups) as g:
                            for q in range(4):
                                n = (r * ngroups + g) * 4 + q
                                act.wait_ge(look_mm, n + 1)
                                act.wait_ge(relT_mm, n + 1)
                                act.activation(rel_hotT[:, q % 2, :], ps[4][:], ACT.Copy).then_inc(relT_ready, 1)
                if k == 5:
                    settle(act)
                    nc.scalar.preload_act_table_set("natural_log_exp_and_others")

                    def filter_terms(n, b):
                        act.wait_ge(ssp_sum, n + 1)
                        act.wait_ge(f1_mm, n + 5)
                        softplus_terms(ps[4][:], col["bfilt1"], f_buf[:, 0, b, :], f_buf[:, 1, b, :], ssp_parts, n * 2)

                    with act.Fori(0, reps) as r:
                        for q in range(AHEAD):
                            filter_terms(act.snap(r * nq + q), q)
                        with act.Fori(0, ngroups) as g:
                            n0 = act.snap((r * ngroups + g) * 4)
                            base = act.snap(tiles_before(reps, 6) + n0 * QUAD)
                            for q in range(4):
                                act.wait_ge(pick_mm, n0 + (q + 3))
                                act.wait_ge(msg_ready, n0 + (q + 3))
                                act.activation(picked[:, q % 2, :], ps[5][:], ACT.Copy).then_inc(pick_ready, 1)
                                filter_terms(act.snap(r * nq + g * 4 + (q + AHEAD)), q % 2)
                                act.wait_ge(sums_free, n0 * 4 + 4 * (q + 1))
                                act.wait_ge(mm_done, base + (GROUP + QUAD * (q + 1)))
                                act.activation(sums[:, q, :], ps[q][:], ACT.Copy).then_inc(add_done, QUAD)

        @block.tensor
        def _(pe):
            pe.wait_ge(made, 13)
            pe.wait_ge(loaded, 16 * n_loads)
            pe.wait_ge(bad_ready, 1)
            pe.matmul(ps[7][:, 0:1], ones[:], reps_f[:, 3:4], start=True, stop=True).then_inc(bad_sum, 1)
            pe.sem_inc(mm_done, GROUP)
            pe.sem_inc(f1_mm, 4)
            pe.sem_inc(look_mm, 2)
            pe.sem_inc(pick_mm, 2)
            pe.sem_inc(filt_mm, 1)
            pe.sem_inc(aggT_mm, 2)
            for s in (out_mm, tab_mm):
                pe.sem_inc(s, 1)
            reps = reps_of(pe)

            def quad_products(base, q, lhs, m, rhs=hot, summed=True):
                pe.wait_ge(add_done, base + QUAD * (q + 1))
                pe.wait_ge(hot_ready, base + QUAD * (q + 1))
                for u in range(QUAD * q, QUAD * (q + 1)):
                    j = u % QUAD
                    o = ps[q][0:m, 0:P] if summed else ps[q][0:m, j * P:(j + 1) * P]
                    pe.matmul(o, lhs[:, u, :], rhs[:, u, :], start=j == 0 or not summed, stop=j == QUAD - 1 or not summed
                              ).then_inc(mm_done, 1)

            def gathered(base, q):
                pe.wait_ge(row_in[q], base + 64)

            def run_pass(pn):
                kind = PASSES[pn]
                if kind == LOOKUP:
                    pe.wait_ge(inv_ready, 1)
                    pe.wait_ge(inv_in, 48)
                def first_product(r, q, g=0, turn=0):
                    per_repeat = ngroups + (q < AHEAD)
                    pe.wait_ge(feat_in[q], r * (16 * per_repeat) + g * 16 + 16 * (turn + 1))
                    pe.wait_ge(ssp_parts, r * nq + g * 4 + (turn * 4 + q + 1))
                    pe.matmul(ps[4][:], wfilt1[:], feat[:, q, :], start=True, stop=True).then_inc(f1_mm, 1)

                def filter_product(r, n, b):
                    pe.wait_ge(ssp_sum, r * nq + n + 3)
                    pe.wait_ge(msg_ready, r * (4 * ngroups) + n + 3)
                    pe.matmul(ps[6 + b][:], ones_b[:], bfilt2_quad[:], start=True, stop=False)
                    for j in range(QUAD):
                        mm = pe.matmul(ps[6 + b][:, j * P:(j + 1) * P], f_buf[:, 2, b, j * P:(j + 1) * P], W["wfilt2"][:],
                                       start=False, stop=j == QUAD - 1)
                    mm.then_inc(filt_mm, 1)

                with pe.Fori(0, reps) as r:
                    if kind == FILTER:
                        for q in range(AHEAD):
                            first_product(r, q)
                        filter_product(r, 0, 0)
                    if kind == LOOKUP:
                        pe.wait_ge(win_ready, reps * pn + r + 1)
                        settle(pe)
                    with pe.Fori(0, ngroups) as g:
                        base = pe.snap(reps * (pn * ntiles) + r * ntiles + g * GROUP)
                        quads = pe.snap((r * ngroups + g) * 4)
                        if kind in (LOOKUP, PLAIN):
                            landed = pe.snap(((reps * (pn - 1) + r) * ngroups + g) * 64)
                        if kind == COUNT:
                            pe.wait_ge(rel_ready, r * ngroups + g + 1)
                            for q in range(4):
                                quad_products(base, q, rel_hot, NCNT, hot_b)
                        if kind == PLAIN:
                            for q in range(4):
                                gathered(landed, q)
                                quad_products(base, q, rows, P)
                        if kind == LOOKUP:
                            pe.wait_ge(rel_ready, reps * ngroups + (r * ngroups + g) * 3 + 3)

                            def transpose_relations(q):
                                pe.wait_ge(relT_ready, quads + (q + 1))
                                for j in range(QUAD):
                                    mm = pe.matmul(ps[4][:, j * P:(j + 1) * P], rel_hot3[:, QUAD * q + j, :],
                                                   ident_b[:], start=True, stop=True)
                                mm.then_inc(relT_mm, 1)

                            def look_up(q):
                                window = inv3[:, bass.ds(win[q], P)]
                                pe.wait_ge(relT_ready, quads + (q + 2))
                                pe.wait_ge(hot_ready, base + QUAD * (q - 1) if q else base)
                                pe.wait_ge(deg_done, quads + (q + 1))
                                pe.matmul(ps[7][:, 0:P], sel_deg[:], window, start=True, stop=True)
                                for j in range(QUAD):
                                    mm = pe.matmul(ps[5 + q % 2][:, j * P:(j + 1) * P],
                                                   rel_hotT[:, q % 2, j * P:(j + 1) * P], window, start=True, stop=True)
                                mm.then_inc(look_mm, 1)

                            win = windows(pe, g)
                            transpose_relations(0)
                            look_up(0)
                            transpose_relations(1)
                            for q in range(4):
                                if q + 1 < 4:
                                    look_up(q + 1)
                                if q + 2 < 4:
                                    transpose_relations(q + 2)
                                gathered(landed, q)
                                quad_products(base, q, rows, P)
                        if kind == FILTER:
                            for q in range(4):
                                pe.wait_ge(hotT_ready, quads + (q + 3))
                                pe.wait_ge(nodes_in[q % 2], quads * 8 + 16 * (q // 2 + 1))
                                pe.wait_ge(pick_ready, quads + (q + 1))
                                for j in range(QUAD):
                                    mm = pe.matmul(ps[5][:, j * P:(j + 1) * P], hotT[:, q % 2, j * P:(j + 1) * P],
                                                   nodes[:, q % 2, :], start=True, stop=True)
                                mm.then_inc(pick_mm, 1)
                                first_product(r, (q + AHEAD) % 4, g, (q + AHEAD) // 4)
                                filter_product(r, g * 4 + (q + 1), (q + 1) % 2)
                                pe.wait_ge(msg_ready, quads + (q + 5))
                                quad_products(base, q, same, P, msg, summed=False)

            run_pass(0)
            for k, p in enumerate(DENSE):
                nck = n_chunks(p)
                hT = hT_s if has_ln(p) else yT
                pe.wait_ge(add_done, tiles_before(reps, k + 1) + GROUP)
                settle(pe)
                if k == 1:
                    pe.wait_ge(wrel2_in, 16)

                def update(i):
                    pe.wait_ge(x_new, i + (turns(k, has_x) + 1))
                    for j in range(4):
                        o = ps[0][:, j * P:(j + 1) * P]
                        if "row" in p:
                            pe.matmul(o, ones[0:1, :], bias_row[p["row"]][:], start=True, stop=False)
                        mm = pe.matmul(o, yT[:, j * P:(j + 1) * P], W[p["upd"]][:], start="row" not in p, stop=True)
                    mm.then_inc(upd_mm, 1)

                def body(f, l, b=0, uses=0):
                    if p["src"] == "sum":
                        if f is not None:
                            pe.wait_ge(agg_step, f * 3 + 3)
                            pe.wait_ge(y_copy, f + 1)
                            for j in range(4):
                                mm = pe.matmul(ps[1][:, j * P:(j + 1) * P], agg_in[:, b, 0, j, :], ident[:],
                                               start=True, stop=True)
                            mm.then_inc(aggT_mm, 1)
                        if l is not None:
                            pe.wait_ge(y_sum, l + 2)
                            update(l)
                        if f is not None:
                            pe.wait_ge(y_copy, f + 2)
                            pe.wait_ge(out_parts, f + 1)
                            pe.matmul(ps[7][:], W["wout1"][:], flat(h), start=True, stop=True).then_inc(out_mm, 1)
                        return
                    if f is not None and has_upd(p):
                        pe.wait_ge(y_ready, f + (turns(k, has_src) + 1))
                        update(f)
                    if l is None:
                        return
                    if has_ln(p):
                        n = turns(k, has_ln)
                        pe.wait_ge(h_ready, l + (n + 1))
                        pe.wait_ge(hT_ready, l + (n + 1))
                        for j in range(4):
                            mm = pe.matmul(ps[1][:, j * P:(j + 1) * P], h[:, j, :], ident[:], start=True, stop=True)
                        mm.then_inc(hT_mm, 1)
                        pe.wait_ge(hT_ready, l + (n + 2))
                    elif has_table(p):
                        pe.wait_ge(y_ready, l + (turns(k, has_src) + 1))
                    if has_root(p):
                        pe.wait_ge(acc_init, l + (turns(k, has_root) + 1))
                        pe.matmul(ps[2][:], W[p["root"]][:], hT[:], start=True, stop=True).then_inc(root_mm, 1)
                    for c in range(nck):
                        j, cut = c // len(cuts(p)), cuts(p)[c % len(cuts(p))]
                        pe.wait_ge((evac_a, evac_v)[c % 2], l * (nck // 2) + (chunks(k) // 2 + c // 2 + 1))
                        pe.matmul(ps[3 + c % 4][:, 0:cut[1] - cut[0]], hT[:, j * P:(j + 1) * P],
                                  W[p["table"]][:, cut[0]:cut[1]], start=True, stop=True).then_inc(tab_mm, 1)

                superblocks(pe, p, body)
                if has_table(p):
                    pe.wait_ge(evac_a, 2 + chunks(k + 1) // 2)
                    pe.wait_ge(evac_v, 2 + chunks(k + 1) // 2)
                    pe.wait_ge(acc_init, turns(k + 1, has_root) + 1)
                    pe.wait_ge(x_new, turns(k + 1, has_x) + 1)
                    run_pass(k + 1)

        @block.vector
        def _(dve):
            dve.sem_inc(evac_v, 2)
            steps = [0]

            def step(ins):
                steps[0] += 1
                ins.then_inc(prep, 1)
                dve.wait_ge(prep, steps[0])

            step(dve.memset(scratch[:, 0:nacc], 0.0))
            step(dve.memset(rel_hot[:], 1.0))
            step(dve.memset(wt_a[:], 0.0))
            step(dve.memset(wt_deg[:], 0.0))
            dve.wait_ge(made, 13)
            step(dve.tensor_copy(iota[:], iota_i[:]))
            step(dve.tensor_copy(iota_b[:], iota_i[:]))
            step(dve.tensor_copy(ident_b[:], ident[:]))
            step(dve.tensor_copy(dump[:], dump_i[:]))
            step(dve.tensor_scalar(place[:], dump[:], float(nacc), None, ALU.subtract))
            step(dve.tensor_scalar(rev[:], iota[:, 0:NREL], -1.0, float(NREL), ALU.mult, ALU.add))
            for c in range(n_attr):
                n = min(P, ntiles - c * P)
                a, best = attr[:, c % 2, 0:n, :], etype[:, c * P:c * P + n]
                dve.wait_ge(attr_in[c % 2], 16 * (c // 2 + 1))
                step(dve.tensor_reduce(best, a, AX.X, ALU.max))
                step(dve.tensor_tensor(a, a, best.unsqueeze(2).broadcast_to([P, n, NREL]), ALU.is_equal))
                step(dve.tensor_tensor(a, a, rev[:].unsqueeze(1).broadcast_to([P, n, NREL]), ALU.mult))
                dve.tensor_reduce(best, a, AX.X, ALU.max).then_inc(attr_used, 1)
            dve.wait_ge(attr_used, n_attr)
            step(dve.tensor_scalar(etype[:], etype[:], -1.0, float(NREL), ALU.mult, ALU.add))

            dve.wait_ge(loaded, 16 * n_loads)
            step(dve.tensor_tensor(rel_dst[:], dst_i[:], first_i[:], ALU.subtract))
            step(dve.tensor_reduce(reps_f[:, 0:1], rel_dst[:], AX.X, ALU.max))
            step(dve.tensor_reduce(reps_f[:, 1:2], rel_dst[:], AX.X, ALU.min))
            step(dve.tensor_scalar(reps_f[:, 0:1], reps_f[:, 0:1], P - 0.5, None, ALU.is_gt))
            step(dve.tensor_scalar(reps_f[:, 1:2], reps_f[:, 1:2], -0.5, None, ALU.is_lt))
            dve.tensor_tensor(reps_f[:, 3:4], reps_f[:, 0:1], reps_f[:, 1:2], ALU.add).then_inc(bad_ready, 1)
            dve.wait_ge(bad_sum, 1)
            step(dve.tensor_scalar(general, ps[7][:, 0:1], 1.0, None, ALU.min))
            step(dve.tensor_scalar(fast, general, -1.0, 1.0, ALU.mult, ALU.add))
            dve.tensor_scalar(reps_i[:], general, float(nwin - 1), 1.0, ALU.mult, ALU.add).then_inc(reps_ready, 1)
            dve.scalar_tensor_tensor(out=row_i[:], in0=src_i[:], scalar=float(NREL), in1=etype[:],
                                     op0=ALU.mult, op1=ALU.add).then_inc(rows_ready, 1)
            reps = reps_of(dve)
            dve.sem_inc(add_done, GROUP)
            step(dve.memset(ones_b[:], 1.0))
            step(dve.memset(bfilt2_quad[:], 0.0))
            step(dve.tensor_copy(bias_rest[:], bias_row["bfilt2"][:]))
            for k in range(3):
                for j in range(QUAD):
                    step(dve.tensor_copy(bfilt2_quad[k * PART:k * PART + 1, j * P:(j + 1) * P], bias_rest[:]))
                if k < 2:
                    step(dve.tensor_copy(part_b[:], bias_rest[:]))
                    step(dve.tensor_tensor(bias_rest[:], bias_rest[:], part_b[:], ALU.subtract))
            dve.sem_inc(ssp_sum, 2)
            dve.sem_inc(hotT_ready, 2)
            dve.sem_inc(pair_step, 2)
            dve.sem_inc(dup_step, 1)
            dve.sem_inc(msg_ready, 4)
            dve.sem_inc(same_ready, 4)
            for s in (deg_done, x_new, y_sum, dest_ready):
                dve.sem_inc(s, 1)

            def set_windows(pn, r):
                n = dve.snap((reps * pn + r) * 3)
                dve.tensor_tensor(win0[:, 1:2], win0[:, 0:1], general, ALU.mult).then_inc(win_step, 1)
                dve.wait_ge(win_step, n + 1)
                dve.tensor_scalar(rel_dst[:], first_i[:], fast, win0[:, 1:2], ALU.mult, ALU.add).then_inc(win_step, 1)
                dve.wait_ge(win_step, n + 2)
                dve.tensor_copy(win_i[:], rel_dst[0:1, :].rearrange("p (n q) -> p n q", q=QUAD)[:, :, 0]).then_inc(win_ready, 1)
                dve.wait_ge(win_ready, reps * pn + r + 1)
                if PASSES[pn] == FILTER:
                    dve.tensor_scalar(node_id, rel_dst[:].rearrange("p (n q) -> p n q", q=QUAD)[:, :, 0], place[:], None,
                                      ALU.add)
                else:
                    dve.tensor_tensor(rel_dst[:], dst_i[:], rel_dst[:], ALU.subtract)
                dve.tensor_scalar(win0[:, 0:1], win0[:, 0:1], float(P), None, ALU.add).then_inc(win_step, 1)
                dve.wait_ge(win_step, n + 3)
                settle(dve)

            def add_quad(base, win, q, target, m):
                dve.wait_ge(mm_done, base + (GROUP + QUAD * (q + 1)))
                dve.wait_ge(add_done, base + (GROUP + QUAD * q))
                window = target[:, bass.ds(win[q], P)]
                dve.tensor_tensor(window, ps[q][0:m, 0:P], window, ALU.add).then_inc(add_done, QUAD)

            def run_pass(pn):
                kind = PASSES[pn]
                finds_dest = pn == len(PASSES) - 2
                if finds_dest:
                    dve.wait_ge(x_out, 16 * turns(pn, has_xout))
                    dve.wait_ge(hT_mm, turns(pn, has_ln))
                weights = {2: wt_a, 3: wt_a, 4: wt_deg, 5: wt_deg}.get(pn)
                step(dve.memset(win0[:, 0:1], 0.0))
                with dve.Fori(0, reps) as r:
                    set_windows(pn, r)
                    with dve.Fori(0, ngroups) as g:
                        turn = dve.snap((reps * pn + r) * ngroups + g)
                        base = dve.snap(turn * GROUP)
                        quads = dve.snap((r * ngroups + g) * 4)
                        win = windows(dve, g)
                        dve.wait_ge(mm_done, base + GROUP)
                        dve.tensor_copy(rw_st[:, 0, :], rel_dst[:, bass.ds(g * GROUP, GROUP)]).then_inc(rw_staged, 1)
                        if kind in (COUNT, LOOKUP):
                            rel = etype[:, bass.ds(g * GROUP, GROUP)]
                            dve.tensor_copy(rw_st[:, 1, :], rel).then_inc(rw_staged, 1)
                            dve.wait_ge(rw_staged, turn * 2 + 2)
                            if kind == COUNT:
                                dve.tensor_tensor(rel_hot[:, :, 0:NREL],
                                                  rw_st[:, 1, :].unsqueeze(2).broadcast_to([P, GROUP, NREL]),
                                                  iota[:, 0:NREL].unsqueeze(1).broadcast_to([P, GROUP, NREL]), ALU.is_equal
                                                  ).then_inc(rel_ready, 1)
                            else:
                                for k in (1, 2, 3):
                                    dve.tensor_tensor(rel_hot3[:, :, k * PART:k * PART + NREL],
                                                      rw_st[:, 1, :].unsqueeze(2).broadcast_to([P, GROUP, NREL]),
                                                      iota[:, 0:NREL].unsqueeze(1).broadcast_to([P, GROUP, NREL]), ALU.is_equal
                                                      ).then_inc(rel_ready, 1)
                        else:
                            dve.tensor_copy(rw_st[:, 1, :], weights[:, bass.ds(g * GROUP, GROUP)]).then_inc(rw_staged, 1)
                            dve.wait_ge(rw_staged, turn * 2 + 2)

                        def one_hot(u):
                            if kind == PLAIN:
                                dve.tensor_scalar(hot[:, u, :], iota[:], rw_st[:, 0, u:u + 1], rw_st[:, 1, u:u + 1],
                                                  ALU.is_equal, ALU.mult).then_inc(hot_ready, 1)
                            elif kind == COUNT:
                                dve.tensor_scalar(hot_b[:, u, :], iota_b[:], rw_st[:, 0, u:u + 1], None, ALU.is_equal
                                                  ).then_inc(hot_ready, 1)
                            else:
                                dve.tensor_scalar(hot[:, u, :], iota[:], rw_st[:, 0, u:u + 1], None, ALU.is_equal
                                                  ).then_inc(hot_made, 1)

                        def weigh(q, j, w, looked_up, out, sig):
                            u = QUAD * q + j
                            dve.tensor_tensor_reduce(
                                out=out, in0=looked_up, in1=hot[:, u, :], scale=1.0, scalar=0.0,
                                op0=ALU.mult, op1=ALU.add, accum_out=wout_st[:, w, u:u + 1]).then_inc(sig, 1)

                        if kind in (COUNT, PLAIN):
                            target = (counts, NCNT) if kind == COUNT else (acc, P)
                            if finds_dest:
                                dve.wait_ge(dup_step, (r * ngroups + g) * 4 + 1)
                                settle(dve)
                                dve.tensor_copy(src_st[:], src_i[:, bass.ds(g * GROUP, GROUP)]).then_inc(src_staged, 1)
                                dve.wait_ge(src_staged, r * ngroups + g + 1)
                            for q in range(4):
                                if finds_dest:
                                    dve.wait_ge(src_in[q], (r * ngroups + g) * 16 + 16)
                                    dve.wait_ge(pair_step, (quads + q) * 2 + 2)
                                    for j in range(QUAD):
                                        u = QUAD * q + j
                                        i = dve.tensor_scalar(pairs[:, j, :], src_row[:, q, j * P:(j + 1) * P],
                                                              src_st[:, u:u + 1], None, ALU.is_equal)
                                    i.then_inc(pair_step, 1)
                                for j in range(QUAD):
                                    one_hot(QUAD * q + j)
                                if finds_dest:
                                    dve.wait_ge(pair_step, (quads + q) * 2 + 3)
                                    dve.sem_inc(same_ready, 1)
                                    for j in range(QUAD):
                                        u = QUAD * q + j
                                        i = dve.tensor_tensor_reduce(
                                            out=pairs_junk[:, j, :], in0=pairs[:, j, :], in1=lower[:], scale=1.0,
                                            scalar=0.0, op0=ALU.mult, op1=ALU.add, accum_out=dup[:, 0, u:u + 1])
                                    i.then_inc(pair_step, 1)
                                if q >= 1 and kind == COUNT:
                                    add_quad(base, win, q - 1, *target)
                            for q in range(3 if kind == COUNT else 0, 4):
                                add_quad(base, win, q, *target)
                            if finds_dest:
                                done = (r * ngroups + g) * 4
                                dve.tensor_scalar(dup[:, 1, :], src_st[:], -1.0, dump[:], ALU.mult, ALU.add).then_inc(dup_step, 1)
                                dve.wait_ge(pair_step, quads * 2 + 10)
                                dve.tensor_scalar(dup[:, 0, :], dup[:, 0, :], 1.0, None, ALU.min).then_inc(dup_step, 1)
                                dve.wait_ge(dup_step, done + 3)
                                dve.tensor_tensor(dup[:, 2, :], dup[:, 0, :], dup[:, 1, :], ALU.mult).then_inc(dup_step, 1)
                                dve.wait_ge(dup_step, done + 4)
                                dve.tensor_tensor(dest[:, bass.ds(g * GROUP, GROUP)], src_st[:], dup[:, 2, :], ALU.add
                                                  ).then_inc(dup_step, 1)
                        if kind == LOOKUP:
                            for u in range(GROUP):
                                one_hot(u)
                            dve.wait_ge(hot_made, (r * ngroups + g) * GROUP + GROUP)

                            def weigh_relation(q):
                                dve.wait_ge(deg_step, quads * QUAD + QUAD * (q + 1))
                                dve.sem_inc(deg_done, 1)
                                for j in range(QUAD):
                                    weigh(q, j, 0, ps[5 + q % 2][:, j * P:(j + 1) * P], hot[:, QUAD * q + j, :], hot_ready)

                            for q in range(4):
                                dve.wait_ge(look_mm, quads + (q + 3))
                                for j in range(QUAD):
                                    weigh(q, j, 1, ps[7][:, 0:P], junk[:, j, :], deg_step)
                                if q >= 2:
                                    add_quad(base, win, q - 2, acc, P)
                                weigh_relation(q)
                            add_quad(base, win, 2, acc, P)
                            add_quad(base, win, 3, acc, P)
                        if kind == LOOKUP:
                            dve.wait_ge(hot_ready, base + GROUP)
                            for full, w in ((wt_a, 0), (wt_deg, 1)):
                                part = full[:, bass.ds(g * GROUP, GROUP)]
                                dve.tensor_tensor(part, wout_st[:, w, :], part, ALU.add)

            def filter_pass():

                def terms_sum(n, b):
                    dve.wait_ge(ssp_parts, n + 2)
                    dve.tensor_tensor(f_buf[:, 2, b, :], f_buf[:, 0, b, :], f_buf[:, 1, b, :], ALU.add).then_inc(ssp_sum, 1)

                step(dve.memset(win0[:, 0:1], 0.0))
                with dve.Fori(0, reps) as r:
                    set_windows(6, r)
                    terms_sum(dve.snap(r * nq), 0)
                    with dve.Fori(0, ngroups) as g:
                        turn = dve.snap(r * ngroups + g)
                        base = dve.snap(tiles_before(reps, 6) + turn * GROUP)
                        dve.wait_ge(dest_ready, turn * 4 + 1)
                        dve.wait_ge(msg_ready, turn * 4 + 4)
                        settle(dve)
                        dve.tensor_copy(rw_st[:, 0, :], src_i[:, bass.ds(g * GROUP, GROUP)]).then_inc(rw_staged, 1)
                        dve.tensor_copy(rw_st[:, 1, :], wt_a[:, bass.ds(g * GROUP, GROUP)]).then_inc(rw_staged, 1)
                        dve.tensor_copy(node_st[:], node_id[:, bass.ds(g * QUAD, QUAD)]).then_inc(rw_staged, 1)
                        dve.wait_ge(rw_staged, reps * (12 * ngroups) + turn * 3 + 3)
                        for q in range(4):
                            filter_quad(r, g, dve.snap(turn * 4 + q), base, q, terms_sum)
                    dve.wait_ge(filt_mm, r * (4 * ngroups + 1) + (4 * ngroups + 1))
                    for q in range(1, AHEAD):
                        terms_sum(r * nq + (4 * ngroups + q), q)

            def filter_quad(r, g, n, base, q, terms_sum):
                us = range(QUAD * q, QUAD * (q + 1))
                quad = slice(QUAD * q, QUAD * (q + 1))
                dve.wait_ge(dst_in[q % 2], n * 8 + (16 * (q // 2 + 1) - 8 * q))
                dve.wait_ge(pick_mm, n + 1)
                dve.tensor_scalar(hotT[:, q % 2, :], dst_row[:, q % 2, :], node_st[:, q:q + 1], None, ALU.is_equal
                                  ).then_inc(hotT_ready, 1)
                dve.wait_ge(filt_mm, r * (4 * ngroups + 1) + g * 4 + (q + 1))
                terms_sum(r * nq + g * 4 + (q + 1), (q + 1) % 2)
                dve.wait_ge(src_in[q], reps * (16 * ngroups) + n * 4 + (16 - 4 * q))
                dve.wait_ge(mm_done, base + QUAD * (q + 1))
                for u in us:
                    j = u % QUAD
                    dve.tensor_scalar(same[:, u, :], src_row[:, q, j * P:(j + 1) * P], rw_st[:, 0, u:u + 1],
                                      None, ALU.is_equal).then_inc(hot_ready, 1)
                dve.wait_ge(sums_free, n * 4 + 4)
                settle(dve)
                dve.tensor_copy(sum_row[:, quad], dest[:, bass.ds(g * GROUP + QUAD * q, QUAD)]).then_inc(dest_ready, 1)
                dve.wait_ge(filt_mm, r * (4 * ngroups + 1) + g * 4 + (q + 2))
                dve.wait_ge(pick_ready, n + 2)
                for u in us:
                    j = u % QUAD
                    i = dve.scalar_tensor_tensor(out=msg[:, u, :], in0=ps[6 + q % 2][:, j * P:(j + 1) * P],
                                                 scalar=rw_st[:, 1, u:u + 1], in1=picked[:, q % 2, j * P:(j + 1) * P],
                                                 op0=ALU.mult, op1=ALU.mult)
                i.then_inc(msg_ready, 1)
                dve.wait_ge(hot_ready, base + QUAD * (q + 1))
                dve.sem_inc(same_ready, 1)

            run_pass(0)
            dve.wait_ge(add_done, reps * ntiles + GROUP)
            dve.wait_ge(counts_out, 16)
            dve.memset(inv3[0:PART, :], 0.0).then_inc(inv_ready, 1)
            dve.wait_ge(wide_in, 16)
            step(dve.tensor_scalar(wide, wide, 1.0, None, ALU.max))
            step(dve.reciprocal(wide, wide))
            for k in range(3):
                last = dve.tensor_copy(wide_part[k], wide)
                if k < 2:
                    step(last)
                    step(dve.tensor_tensor(wide, wide, wide_part[k], ALU.subtract))
            last.then_inc(parts_ready, 1)
            for k, p in enumerate(DENSE):
                nck = n_chunks(p)
                if p["src"] == "bn":
                    dve.wait_ge(add_done, tiles_before(reps, k + 1) + GROUP)
                    step(dve.tensor_scalar(acc[:, 0:n_nodes], acc[:, 0:n_nodes], 0.0, None, ALU.max))
                    for c in range(n_nodes // bn_chunk):
                        last = dve.bn_stats(bn_st[:, c, :], acc[:, c * bn_chunk:(c + 1) * bn_chunk])
                    step(last)
                    step(dve.bn_aggr(bn[:, 0:2], bn_st[:]))
                    dve.tensor_scalar(bn[:, 2:3], bn[:, 1:2], EPS, None, ALU.add).then_inc(bn_var, 1)
                    dve.wait_ge(bn_sd, 1)
                    step(dve.reciprocal(bn[:, 4:5], bn[:, 3:4]))
                    step(dve.tensor_tensor(bn[:, 5:6], bn[:, 4:5], col["gamma"], ALU.mult))
                    step(dve.tensor_tensor(bn[:, 7:8], bn[:, 0:1], bn[:, 5:6], ALU.mult))
                    dve.tensor_tensor(bn[:, 6:7], col["beta"], bn[:, 7:8], ALU.subtract).then_inc(bn_ready, 1)

                def body(f, l, b=0, uses=0):
                    if p["src"] == "sum":
                        if f is not None:
                            dve.wait_ge(agg_read[b], uses * 64 + 64)
                            for n, (to, other) in enumerate(((0, 1), (2, 3), (0, 2))):
                                if n == 2:
                                    dve.wait_ge(agg_step, f * 3 + 2)
                                dve.tensor_tensor(agg_in[:, b, to], agg_in[:, b, to], agg_in[:, b, other], ALU.add
                                                  ).then_inc(agg_step, 1)
                        if l is None:
                            return
                        dve.wait_ge(out_parts, l + 2)
                        dve.tensor_tensor(yT[:], hT_s[:], tab_s[:, 0, 0:SB], ALU.add).then_inc(y_sum, 1)
                        f = l
                    if f is not None and has_x(p):
                        dve.wait_ge(x_in, f * 16 + 16 * (turns(k, has_x) + 1))
                        dve.wait_ge(x_out, f * (16 * has_xout(p)) + 16 * turns(k, has_xout))
                        if has_ln(p):
                            dve.wait_ge(h_ready, f + turns(k, has_ln))
                        if has_upd(p):
                            dve.wait_ge(upd_mm, f + (turns(k, has_upd) + 1))
                            dve.tensor_tensor(flat(xn), ps[0][:], flat(xs), ALU.add).then_inc(x_new, 1)
                        else:
                            dve.tensor_copy(flat(xn), flat(xs)).then_inc(x_new, 1)
                    if f is not None and has_ln(p):
                        n = turns(k, has_ln)
                        dve.wait_ge(x_new, f + (turns(k, has_x) + 2))
                        for j in range(4):
                            dve.bn_stats(st[:, j, :], xn[:, j, :]).then_inc(st_ready, 1)
                        dve.wait_ge(st_ready, f * 4 + (4 * n + 4))
                        settle(dve)
                        for j in range(4):
                            dve.bn_aggr(mv[:, j, :], st[:, j, :]).then_inc(mv_ready, 1)
                        dve.wait_ge(mv_ready, f * 4 + (4 * n + 4))
                        dve.tensor_scalar(nrm[:, :, 0], mv[:, :, 1], EPS, None, ALU.add).then_inc(var_ready, 1)
                        dve.wait_ge(sd_ready, f + (n + 1))
                        dve.reciprocal(nrm[:, :, 2], nrm[:, :, 1]).then_inc(rstd_ready, 1)
                        dve.wait_ge(rstd_ready, f + (n + 1))
                        dve.scalar_tensor_tensor(out=nrm[:, :, 3], in0=mv[:, :, 0], scalar=-1.0, in1=nrm[:, :, 2],
                                                 op0=ALU.mult, op1=ALU.mult).then_inc(nrm_ready, 1)
                    if l is None:
                        return
                    for c in range(1, nck, 2):
                        j, cut = c // len(cuts(p)), cuts(p)[c % len(cuts(p))]
                        dve.wait_ge(tab_mm, l * nck + (chunks(k) + c + 2))
                        wait_lane(dve, k, l, j)
                        dve.tensor_copy(staged(p, j, *cut), ps[3 + c % 4][:, 0:cut[1] - cut[0]]
                                        ).then_inc(evac_v, 1)

                superblocks(dve, p, body)
                if k == 2:
                    dve.wait_ge(late_in, 32)
                    dve.scalar_tensor_tensor(out=row_i[:], in0=src_i[:], scalar=3.0, in1=etype[:, :].bitcast(I32),
                                             op0=ALU.mult, op1=ALU.add).then_inc(rows_ready, 1)
                if k == 3:
                    dve.tensor_copy(row_i[:], src_i[:]).then_inc(rows_ready, 1)
                if k == 5:
                    wait_stores(dve, k)
                    dve.wait_ge(y_ready, turns(k + 1, has_src))
                    filter_pass()
                elif has_table(p):
                    if has_root(p):
                        dve.wait_ge(acc_init, turns(k + 1, has_root) + 1)
                    else:
                        dve.wait_ge(y_ready, turns(k + 1, has_src))
                        dve.memset(acc[:], 0.0)
                    wait_stores(dve, k)
                    if PASSES[k + 1] == LOOKUP:
                        dve.wait_ge(hT_mm, turns(k + 1, has_ln))
                        step(dve.memset(xn_h[:], 0.0))
                    run_pass(k + 1)


def kernel(**inputs):
    import concourse.bacc as bacc
    from concourse.bass_utils import run_bass_kernel_spmd

    a = {n: np.asarray(v) for n, v in inputs.items()}
    n_nodes, n_edges = a["x"].shape[0], a["src"].shape[0]
    nacc = -(-(n_nodes + P) // SB) * SB
    ntiles = -(-n_edges // (GROUP * P)) * GROUP
    pad = ntiles * P - n_edges

    def per_edge(v, fill):
        return np.concatenate([v, np.full(pad, fill, v.dtype)]).reshape(ntiles, P).T

    dst = per_edge(a["dst"], n_nodes)
    attr = np.concatenate([a["edge_attr_42"][:, 16:26], np.zeros((pad, 10), np.float32)])
    feat = np.concatenate([a["edge_attr_20"], np.zeros((pad + AHEAD * BANK, 20), np.float32)])
    rel = lambda w: w.transpose(1, 0, 2).reshape(w.shape[1], -1)
    vectors = ["L0_gnn_b1", "L0_gnn_b2", "L2_gnn_bl1", "L2_gnn_bl2", "L2_gnn_gamma", "L2_gnn_beta",
               "L3_gnn_b_filt1", "L3_gnn_b_out1"]
    laid = dict(
        dst_row=np.ascontiguousarray(dst.T).reshape(1, -1),
        x=np.concatenate([a["x"], np.zeros((nacc - n_nodes, a["x"].shape[1]), np.float32)]),
        src=per_edge(a["src"], 0), src_row=np.concatenate([a["src"], np.zeros(pad, np.int32)])[None], dst=dst,
        first=np.broadcast_to(np.repeat(dst[0:1, ::QUAD], QUAD, 1), dst.shape),
        type=per_edge(a["edge_type_3"], 0), weight=per_edge(a["edge_weight"], 0),
        attr=attr.reshape(ntiles, P, 10).transpose(1, 0, 2), feat=feat.T,
        wrel=rel(a["L0_gnn_w_rel1"]), wrel2=rel(a["L0_gnn_w_rel2"]), root1=a["L0_gnn_root1"], root2=a["L0_gnn_root2"],
        w1=rel(a["L1_gnn_weight"]), wl1=a["L2_gnn_Wl1"].T, wr1=a["L2_gnn_Wr1"].T, wl2=a["L2_gnn_Wl2"].T,
        wr2=a["L2_gnn_Wr2"].T, fcw=a["L2_gnn_fcW"].T, win=a["L3_gnn_W_in2f"], wout1=a["L3_gnn_W_out1"],
        wout2=a["L3_gnn_W_out2"], wfilt2=a["L3_gnn_W_filt2"], wfilt1=a["L3_gnn_W_filt1"],
        cols=np.stack([a[v] for v in vectors], 1), fcb=a["L2_gnn_fcb"][None], bout2=a["L3_gnn_b_out2"][None],
        bfilt2=a["L3_gnn_b_filt2"][None])

    nc = bacc.Bacc("TRN2", target_bir_lowering=False, num_devices=1)
    arrays, handles = {}, {}
    for name, v in laid.items():
        arrays[f"in_{name}"] = v = np.ascontiguousarray(v)
        handles[name] = nc.dram_tensor(f"in_{name}", v.shape, mybir.dt.from_np(v.dtype), kind="ExternalInput").ap()
    out = nc.dram_tensor("out_x", (nacc, P), F32, kind="ExternalOutput").ap()
    build(nc, handles, out, n_nodes, n_edges)
    got = run_bass_kernel_spmd(nc, [arrays], core_ids=[0])
    return got.results[0]["out_x"][:n_nodes]
```
